# Optimizing a Trainium2 kernel written in Bass

```python
import numpy as np
import jax
import jax.numpy as jnp

def _softmax(x, axis=-1):
    return jax.nn.softmax(x, axis=axis)

def _gelu(x):
    return jax.nn.gelu(x, approximate=True)

def _silu(x):
    return jax.nn.silu(x)

def _sigmoid(x):
    return jax.nn.sigmoid(x)

def _layernorm(x, axis=-1, eps=1e-05):
    m = jnp.mean(x, axis=axis, keepdims=True)
    v = jnp.var(x, axis=axis, keepdims=True)
    return (x - m) / jnp.sqrt(v + eps)

def _scatter_add(tgt, idx, src, axis=0):
    return tgt.at[idx].add(src)

def _segment_sum(src, seg, n):
    return jax.ops.segment_sum(src, seg, n)
kernel_name = 'mk_xattn_ffn_d1_seqx_r8_d71348'

def setup_inputs(seed: int=0):
    np.random.seed(seed)
    _w = jnp.asarray

    def _rec_inputs():
        import jax
        import jax.numpy as jnp
        _rk = jax.random.key(seed)
        x = -0.0002928 + 1 * jax.random.normal(jax.random.fold_in(_rk, 1), (1, 1024, 128), jnp.float32)
        _lenS = 1024 - jax.random.randint(jax.random.fold_in(_rk, 7), (1,), 0, max(1, 1024 // 4) + 1, jnp.int32)
        _lenS2 = 6404 - jax.random.randint(jax.random.fold_in(_rk, 8), (1,), 0, max(1, 6404 // 4) + 1, jnp.int32)
        _ctx_1024P = jax.random.normal(jax.random.fold_in(_rk, 11), (1, 16, 128), jnp.float32)
        _ctx_1024c = jax.random.dirichlet(jax.random.fold_in(_rk, 511), 0.3 * jnp.ones((16,), jnp.float32), (1, 6404))
        _ctx_1024t = jnp.einsum('bsk,bkd->bsd', _ctx_1024c, _ctx_1024P)
        _ctx_1024t = _ctx_1024t * jax.lax.rsqrt(jnp.mean(jnp.square(_ctx_1024t)) + 1e-12) * 0.953939
        ctx_1024 = -1.39393e-06 + 0.999914 * (_ctx_1024t + 0.3 * jax.random.normal(jax.random.fold_in(_rk, 611), (1, 6404, 128), jnp.float32))
        _validS = jnp.arange(1024)[None, :] < _lenS[:, None]
        _validS2 = jnp.arange(6404)[None, :] < _lenS2[:, None]
        _causal = jnp.tril(jnp.ones((1024, 1024), dtype=bool))
        mask_SxS2_bk1 = jnp.broadcast_to(_validS2[0:1, :], (1024, 6404))
        return (x, ctx_1024, mask_SxS2_bk1)
    x, ctx_1024, mask_SxS2_bk1 = _rec_inputs()

    def _L0_xattn_setup():
        import jax, jax.numpy as jnp
        import numpy as np
        B, S, D, H = (2, 256, 128, 16)
        HW = D // H
        MASK_FILL = -100000000.0
        key0 = jax.random.key(seed)
        ks = jax.random.split(key0, 12)
        inp = {'query': jax.random.normal(ks[0], (B, S, D), jnp.float32), 'key': jax.random.normal(ks[1], (B, S, D), jnp.float32), 'value': jax.random.normal(ks[2], (B, S, D), jnp.float32), 'mask': jax.random.randint(ks[3], (S, S), 0, 2).astype(jnp.bool_), 'Wq': jax.random.normal(ks[4], (H, HW, D), jnp.float32) * 0.02, 'bq': jnp.zeros((H, HW), jnp.float32), 'Wk': jax.random.normal(ks[5], (H, HW, D), jnp.float32) * 0.02, 'bk': jnp.zeros((H, HW), jnp.float32), 'Wv': jax.random.normal(ks[6], (H, HW, D), jnp.float32) * 0.02, 'bv': jnp.zeros((H, HW), jnp.float32), 'Wo': jax.random.normal(ks[7], (D, H, HW), jnp.float32) * 0.02, 'bo': jnp.zeros((D,), jnp.float32)}
        return inp
    _L0_xattn_all = _L0_xattn_setup()
    _L0_xattn_in = {k: v for k, v in _L0_xattn_all.items() if k in ('Wq', 'bq', 'Wk', 'bk', 'Wv', 'bv', 'Wo', 'bo')}
    del _L0_xattn_all

    def _L0_ffn_setup():
        import jax, jax.numpy as jnp
        import numpy as np
        H, I, E_ROUTED, TOP_K = (128, 352, 7, 2)
        B, S = (4, 256)

        def _expert(h, g, u, d):
            return jnp.einsum('...i,hi->...h', jax.nn.silu(h @ g.T) * (h @ u.T), d)
        key = jax.random.key(seed)
        ks = jax.random.split(key, 10)
        sc = 0.02
        return {'x': jax.random.normal(ks[0], (B, S, H), dtype=jnp.float32), 'sg': jax.random.normal(ks[1], (I, H), dtype=jnp.float32) * sc, 'su': jax.random.normal(ks[2], (I, H), dtype=jnp.float32) * sc, 'sd': jax.random.normal(ks[3], (H, I), dtype=jnp.float32) * sc, 'rg': jax.random.normal(ks[4], (E_ROUTED, I, H), dtype=jnp.float32) * sc, 'ru': jax.random.normal(ks[5], (E_ROUTED, I, H), dtype=jnp.float32) * sc, 'rd': jax.random.normal(ks[6], (E_ROUTED, H, I), dtype=jnp.float32) * sc, 'wr': jax.random.normal(ks[7], (E_ROUTED, H), dtype=jnp.float32) * sc, 'rb': jnp.zeros((E_ROUTED,), dtype=jnp.float32)}
    _L0_ffn_all = _L0_ffn_setup()
    _L0_ffn_in = {k: v for k, v in _L0_ffn_all.items() if k in ('sg', 'su', 'sd', 'rg', 'ru', 'rd', 'wr', 'rb')}
    del _L0_ffn_all
    return {'x': x, 'ctx_1024': ctx_1024, 'mask_SxS2_bk1': mask_SxS2_bk1, 'L0_xattn_Wq': _L0_xattn_in['Wq'], 'L0_xattn_bq': _L0_xattn_in['bq'], 'L0_xattn_Wk': _L0_xattn_in['Wk'], 'L0_xattn_bk': _L0_xattn_in['bk'], 'L0_xattn_Wv': _L0_xattn_in['Wv'], 'L0_xattn_bv': _L0_xattn_in['bv'], 'L0_xattn_Wo': _L0_xattn_in['Wo'], 'L0_xattn_bo': _L0_xattn_in['bo'], 'L0_ffn_sg': _L0_ffn_in['sg'], 'L0_ffn_su': _L0_ffn_in['su'], 'L0_ffn_sd': _L0_ffn_in['sd'], 'L0_ffn_rg': _L0_ffn_in['rg'], 'L0_ffn_ru': _L0_ffn_in['ru'], 'L0_ffn_rd': _L0_ffn_in['rd'], 'L0_ffn_wr': _L0_ffn_in['wr'], 'L0_ffn_rb': _L0_ffn_in['rb']}

def reference(x, ctx_1024, mask_SxS2_bk1, L0_xattn_Wq, L0_xattn_bq, L0_xattn_Wk, L0_xattn_bk, L0_xattn_Wv, L0_xattn_bv, L0_xattn_Wo, L0_xattn_bo, L0_ffn_sg, L0_ffn_su, L0_ffn_sd, L0_ffn_rg, L0_ffn_ru, L0_ffn_rd, L0_ffn_wr, L0_ffn_rb):
    import jax
    import jax.numpy as jnp

    def _L0_xattn_ref(query, key, value, mask, Wq, bq, Wk, bk, Wv, bv, Wo, bo):
        import jax, jax.numpy as jnp
        import numpy as np
        B, S, D, H = (2, 256, 128, 16)
        HW = D // H
        MASK_FILL = -100000000.0
        q = jnp.einsum('bsd,hwd->bhsw', query, Wq) + bq[:, None, :]
        k = jnp.einsum('btd,hwd->bhtw', key, Wk) + bk[:, None, :]
        v = jnp.einsum('btd,hwd->bhtw', value, Wv) + bv[:, None, :]
        logits = jnp.einsum('bhsw,bhtw->bhst', q, k)
        logits = jnp.where(mask, MASK_FILL, logits)
        score = jax.nn.softmax(logits, axis=-1)
        attn = jnp.einsum('bhst,bhtw->bhsw', score, v) / jnp.sqrt(jnp.float32(HW))
        out = jnp.einsum('bhsw,ohw->bso', attn, Wo) + bo
        return out

    def _L0_ffn_ref(x, sg, su, sd, rg, ru, rd, wr, rb):
        import jax, jax.numpy as jnp
        import numpy as np
        H, I, E_ROUTED, TOP_K = (128, 352, 7, 2)
        B, S = (4, 256)

        def _expert(h, g, u, d):
            return jnp.einsum('...i,hi->...h', jax.nn.silu(h @ g.T) * (h @ u.T), d)
        shared_out = _expert(x, sg, su, sd)
        logits = x @ wr.T + rb
        probs = jax.nn.softmax(logits, axis=-1)
        scores, idx = jax.lax.top_k(probs, TOP_K)
        scores = scores / scores.sum(axis=-1, keepdims=True)
        w = jnp.sum(scores[..., None] * jax.nn.one_hot(idx, E_ROUTED, dtype=x.dtype), axis=-2)
        out = shared_out
        for e in range(E_ROUTED):
            out = out + w[..., e:e + 1] * _expert(x, rg[e], ru[e], rd[e])
        return out
    x = x + _L0_xattn_ref(_layernorm(x, axis=-1), ctx_1024, ctx_1024, mask_SxS2_bk1, L0_xattn_Wq, L0_xattn_bq, L0_xattn_Wk, L0_xattn_bk, L0_xattn_Wv, L0_xattn_bv, L0_xattn_Wo, L0_xattn_bo)
    x = x + _L0_ffn_ref(_layernorm(x, axis=-1), L0_ffn_sg, L0_ffn_su, L0_ffn_sd, L0_ffn_rg, L0_ffn_ru, L0_ffn_rd, L0_ffn_wr, L0_ffn_rb)
    return x

_drawn_inputs = setup_inputs


def setup_inputs(seed=0):
    import zlib

    import numpy as np

    out = dict(_drawn_inputs(seed))
    spreads = {'L0_xattn_bq': (0.0, 0.8),
     'L0_xattn_bk': (0.0, 0.8),
     'L0_xattn_bv': (0.0, 0.8),
     'L0_xattn_bo': (0.0, 0.1),
     'L0_ffn_rb': (0.0, 0.8)}
    factors = {'ctx_1024': 7.0,
     'L0_xattn_Wq': 8.0,
     'L0_xattn_Wk': 8.0,
     'L0_xattn_Wv': 6.277,
     'L0_xattn_Wo': 4.663,
     'L0_ffn_sg': 5.295,
     'L0_ffn_su': 4.881,
     'L0_ffn_sd': 4.889,
     'L0_ffn_rg': 8.0,
     'L0_ffn_ru': 8.0,
     'L0_ffn_rd': 8.0,
     'L0_ffn_wr': 8.0}
    for name, (base, spread) in spreads.items():
        noise = np.random.default_rng([zlib.crc32(name.encode()), seed]).standard_normal(out[name].shape)
        drawn = base * np.exp(spread * noise) if base else spread * noise
        out[name] = jnp.asarray(drawn.astype(out[name].dtype))
    for name, factor in factors.items():
        out[name] = (out[name] * factor).astype(out[name].dtype)
    return out
```

```python
from contextlib import ExitStack

import concourse.bass as bass
from concourse import mybir

F32 = mybir.dt.float32
BF16 = mybir.dt.bfloat16
I32 = mybir.dt.int32
U8 = mybir.dt.uint8
ALU = mybir.AluOpType
ACT = mybir.ActivationFunctionType
AX = mybir.AxisListType.X

P = 128
KT = 128
BLK = 2 * KT
HW = 8
PARTS = 3
Q_TERM = (0, 1, 2, 0, 1, 0)
K_TERM = (0, 0, 0, 1, 1, 2)
MASK_ROW = len(Q_TERM) * HW
MAX_ROW = MASK_ROW + 1
ROWS = MAX_ROW + PARTS
HALF = 64
BIG = float(2.0 ** 100)
FLOOR = -1.0e9


def padded_keys(T):
    return -(-T // BLK) * BLK


def xattn_moe(nc, x, ctxT, mask, wqT, bq, wkT, bk, wvT, bv, woT, bo, gu, dn, wrT, rb, out, T):
    S, D = x.shape
    QT = S // P
    QC = S // 512
    TP = ctxT.shape[1]
    NB = TP // BLK
    NT = TP // KT
    H = D // HW
    NP = H // 2
    STAGES = NP + 2
    E, _, I2 = gu.shape
    I = I2 // 2
    ER = E - 1
    ICH = [(o, min(P, I - o)) for o in range(0, I, P)]
    NI = len(ICH)
    assert D == P and QC == 2 and QT == 8 and H == 16 and NI == 3 and E % 2 == 0

    k_scr = nc.dram_tensor("k_scr", (H, MAX_ROW, TP), BF16, kind="Internal").ap()
    v_scr = nc.dram_tensor("v_scr", (NT, KT, H * (HW + 1)), F32, kind="Internal").ap()
    q_scr = nc.dram_tensor("q_scr", (PARTS, D, S), BF16, kind="Internal").ap()
    m_scr = nc.dram_tensor("m_scr", (NP, PARTS, 2 * QT, P), BF16, kind="Internal").ap()

    with ExitStack() as ctx:
        def sb(name, shape, dt=F32):
            return ctx.enter_context(nc.sbuf_tensor(name, shape, dt))

        def sem(name):
            return ctx.enter_context(nc.semaphore(name))

        PS = ctx.enter_context(nc.psum_tensor("PS", [P, 8, 512], F32))
        SM = 4
        OB = 6

        x_sb = sb("x_sb", [P, QT, D])
        mask_sb = sb("mask_sb", [P, QT, TP], U8)
        mask_and = sb("mask_and", [P, TP // 4], I32)
        mask_or = sb("mask_or", [P, TP // 4], I32)
        flags_bf = sb("flags_bf", [P, 2, TP], BF16)
        o_sb = flags_bf[:, :, :].rearrange("p a k -> p (a k)")[:, 0:NP * 1024].bitcast(F32) \
            .rearrange("p (s q) -> p s q", s=NP)
        q_parts = flags_bf[:, 0, 0:PARTS * S].rearrange("p (j q) -> p j q", j=PARTS)
        m_ring = mask_and[:, 0:QT * KT].bitcast(BF16).rearrange("p (b t k) -> p b t k", b=2, t=QT)
        acc = mask_or[:, 0:S].bitcast(F32).rearrange("p (t d) -> p t d", t=QT)
        ctx_all = sb("ctx_all", [P, TP])
        prob = ctx_all[:, 0:4096].rearrange("p (b h q) -> p b h q", b=2, h=2)
        k_parts = sb("k_parts", [P, PARTS, TP], BF16)
        late = k_parts[:, :, :].rearrange("p j k -> p (j k)").bitcast(F32)
        sizes = (2 * NI * 512, 2 * 512, 2 * I2, 2 * NI * D)
        ends = [sum(sizes[:n + 1]) for n in range(4)]
        hid = late[:, 0:ends[0]].rearrange("p (c n q) -> p c n q", c=2, n=NI)
        sg = late[:, ends[0]:ends[1]].rearrange("p (b q) -> p b q", b=2)
        w_gu = late[:, ends[1]:ends[2]].rearrange("p (b i) -> p b i", b=2)
        w_dn = late[:, ends[2]:ends[3]].rearrange("p (b n o) -> p b n o", b=2, n=NI)
        q_st = sb("q_st", [P, NP, S], BF16)
        wq_sb = sb("wq_sb", [P, D])
        wk_sb = sb("wk_sb", [P, D])
        wv_sb = sb("wv_sb", [P, D])
        wo_sb = sb("wo_sb", [P, D])
        wr_sb = sb("wr_sb", [P, ER])
        bq_sb = sb("bq_sb", [P, 1])
        bk_sb = sb("bk_sb", [P, 1])
        bv_sb = sb("bv_sb", [P, D])
        bo_sb = sb("bo_sb", [P, D])
        rb_sb = sb("rb_sb", [P, ER])
        ident = sb("ident", [P, P])
        neg_ident = sb("neg_ident", [P, P], BF16)
        ones_f = sb("ones_f", [P, 1])
        ones_b = sb("ones_b", [P, 1], BF16)
        zeros_b = sb("zeros_b", [P, 512], BF16)
        q_rows = sb("q_rows", [1 + PARTS, S], BF16)
        blk_idx = sb("blk_idx", [1, NB], I32)
        blk_idx_f = sb("blk_idx_f", [1, NB])
        e_rank = sb("e_rank", [P, ER], I32)
        e_rank_f = sb("e_rank_f", [P, ER])
        tmp_a = sb("tmp_a", [P, QT, D])
        tmp_b = sb("tmp_b", [P, QT, D])
        xnT = sb("xnT", [P, S])
        st8 = sb("st8", [P, 6, QT])
        flag = sb("flag", [P, 3, NT])
        row = sb("row", [1, 4, 2 * NB])
        ctl = sb("ctl", [1, 3], I32)
        mrow_bf = sb("mrow_bf", [NT, KT], BF16)
        ctx_blk = sb("ctx_blk", [P, BLK])
        k32 = sb("k32", [P, BLK])
        kr1 = sb("kr1", [P, BLK])
        v_blk = sb("v_blk", [P, 2, H, HW + 1])
        csum = sb("csum", [P, 1])
        csum_b = sb("csum_b", [P, P])
        k_ring = sb("k_ring", [P, 2, 2, KT], BF16)
        v_ring = sb("v_ring", [P, 2, 2 * (HW + 1)])
        tile_max = sb("tile_max", [P, 2, 2 * QT])
        run_max = sb("run_max", [P, 32])
        maxT = sb("maxT", [P, 32])
        max_r = sb("max_r", [P, 32])
        max_p = sb("max_p", [P, PARTS, 32], BF16)
        none_l = sb("none_l", [P, NP * 4 * 4])
        den = sb("den", [P, NP * 4 * 4])
        rt = sb("rt", [P, 6, QT, ER])
        rs = sb("rs", [P, 6, QT])
        w_all = sb("w_all", [P, E, QT])
        w_cur = sb("w_cur", [P, 2, QT])

        x_in = sem("x_in")
        mask_in = [sem(f"mask_in{t}") for t in range(QT)]
        ctx_in = sem("ctx_in")
        small_in = sem("small_in")
        consts = sem("consts")
        dve_step = sem("dve_step")
        act_step = sem("act_step")
        pe_step = sem("pe_step")
        csum_done = sem("csum_done")
        q_stored = sem("q_stored")
        q_stacked = sem("q_stacked")
        q_rows_in = sem("q_rows_in")
        mrow_stored = sem("mrow_stored")
        ctl_ready = sem("ctl_ready")
        ctx_copied = sem("ctx_copied")
        k_mm = sem("k_mm")
        v_mm = sem("v_mm")
        k_split = sem("k_split")
        v_evac = sem("v_evac")
        v_stored = sem("v_stored")
        k_stored = sem("k_stored")
        ring_in = [sem("ring_in0"), sem("ring_in1")]
        tile_done = sem("tile_done")
        mask_tile = sem("mask_tile")
        sc_ready = sem("sc_ready")
        exp_done = sem("exp_done")
        sm_ready = sem("sm_ready")
        max_done = sem("max_done")
        max_init = sem("max_init")
        max_fold = sem("max_fold")
        max_split = sem("max_split")
        max_stored = sem("max_stored")
        max_in = sem("max_in")
        o_evac = sem("o_evac")
        w_in = [sem("w_in0"), sem("w_in1")]
        gu_ready = sem("gu_ready")
        silu_done = sem("silu_done")
        hid_done = sem("hid_done")
        w_copied = sem("w_copied")
        y_ready = sem("y_ready")
        y_used = sem("y_used")
        out_done = sem("out_done")

        N_CONST = 13
        N_SMALL = 10

        def pair_slice(L):
            if L < 2:
                return slice(L, L + 3, 2), None, 0
            if L < NP:
                return slice(L - 2, L + 1, 2), 0, 1
            return slice(L - 4, L - 1, 2), 1, None

        V_XN1 = 8
        V_QPARTS = 13
        V_AND = 26
        V_OR = 28
        V_FLAG = 31
        V_MROW = 32
        V_CSUM = 42
        V_NORM = 49
        V_ATT = 56
        V_ATT_T = 57
        V_XN2 = 66
        V_XN2_T = 67
        V_GAP = 80

        def block_of(it, first):
            return nc.s_assert_within(it + first, 0, NB - 1, skip_runtime_bounds_check_because="it < NB - first")

        block = ctx.enter_context(nc.Block())

        @block.sync
        def _(sp):
            sp.sem_inc(v_stored, 16)
            sp.dma_start(x_sb[:, :, :], x.rearrange("(t p) d -> p t d", p=P)).then_inc(x_in, 16)
            for t in range(QT):
                sp.dma_start(mask_sb[:, t, :], mask[t * P:(t + 1) * P, :]).then_inc(mask_in[t], 16)
                if t == QT // 2 - 1:
                    sp.dma_start(ctx_all[:, :], ctxT).then_inc(ctx_in, 16)

            sp.wait_ge(dve_step, V_QPARTS)
            sp.dma_start(q_scr.rearrange("j r q -> r j q"), q_parts[:, :, :]).then_inc(q_stored, 16)
            sp.wait_ge(q_stored, 16)
            q_src = q_scr.rearrange("j (p h w) q -> j h w p q", h=2, w=HW)
            for h in range(2):
                for t, j in enumerate(Q_TERM):
                    r0 = h * HALF + t * HW
                    sp.dma_start(q_st[r0:r0 + HW, :, :], q_src[j, h]).then_inc(q_stacked, 16)

            sp.wait_ge(dve_step, V_MROW)
            sp.dma_start(k_scr[:, MASK_ROW, :].rearrange("h (t k) -> t h k", k=KT),
                         mrow_bf[:, :].unsqueeze(1).to_broadcast([NT, H, KT])).then_inc(mrow_stored, 16)

            sp.wait_ge(ctl_ready, 1)
            first = sp.value_load(ctl[0:1, 0:1], min_val=0, max_val=NB - 1)
            nblk = sp.value_load(ctl[0:1, 2:3], min_val=1, max_val=NB)
            with sp.Fori(0, nblk) as it:
                blk = block_of(it, first)
                sp.wait_ge(v_evac, it + 2)
                sp.dma_start(v_scr[bass.ds(blk * 2, 2), :, :].rearrange("t k n -> k t n"),
                             v_blk[:, :, :, :].rearrange("p t h w -> p t (h w)")).then_inc(v_stored, 16)
                sp.wait_ge(k_split, it * 5 + (5 + 5))
                for t, j in enumerate(K_TERM):
                    sp.dma_start(k_scr[:, t * HW:(t + 1) * HW, bass.ds(blk * BLK, BLK)],
                                 k_parts[:, j, bass.ds(blk * BLK, BLK)]).then_inc(k_stored, 16)

            k_src = k_scr.rearrange("(p h) r k -> h r p k", h=2)
            for L in range(STAGES):
                pairs, exp_at, _ = pair_slice(L)
                s = max(L - 2, 0)
                with sp.Fori(0, nblk) as it:
                    blk = block_of(it, first)
                    g2 = sp.snap((it + nblk * L) * 2)
                    for b in range(2):
                        sp.wait_ge(tile_done, g2 + (b + 1))
                        for h in range(2):
                            sp.dma_start(k_ring[h * HALF:h * HALF + MAX_ROW, b, :, :],
                                         k_src[h, :, pairs, bass.ds(blk * BLK + b * KT, KT)]) \
                                .then_inc(ring_in[b], 16)
                        n0 = s * 2 * (HW + 1)
                        sp.dma_start(v_ring[:, b, :],
                                     v_scr[bass.ds(blk * 2 + b, 1), :, n0:n0 + 2 * (HW + 1)]
                                     .rearrange("t k n -> k (t n)")).then_inc(ring_in[b], 16)

            def load_expert(e, b):
                sp.dma_start(w_gu[:, b, :], gu[bass.ds(e, 1), :, :].rearrange("e d i -> d (e i)")) \
                    .then_inc(w_in[b], 16)
                sp.dma_start(w_dn[:, b, 0:2, :],
                             dn[bass.ds(e, 1), 0:2 * P, :].rearrange("e (c i) o -> i (e c) o", i=P)) \
                    .then_inc(w_in[b], 16)
                sp.dma_start(w_dn[0:ICH[2][1], b, 2, :],
                             dn[bass.ds(e, 1), 2 * P:I, :].rearrange("e i o -> i (e o)")).then_inc(w_in[b], 16)

            load_expert(0, 0)
            load_expert(1, 1)
            with sp.Fori(0, E // 2 - 1) as i:
                for b in range(2):
                    sp.wait_ge(y_ready, i * 4 + (2 * b + 2 + 2))
                    load_expert(i * 2 + (2 + b), b)
            out_v = out.rearrange("a (t p) d -> p (a t) d", p=P)
            for c in range(QC):
                sp.wait_ge(y_used, 2 * (E - 1) + c + 1 + 2)
                sp.dma_start(out_v[:, 4 * c:4 * c + 4, :], acc[:, 4 * c:4 * c + 4, :]).then_inc(out_done, 16)
            sp.wait_ge(out_done, 16 * QC)

        @block.gpsimd
        def _(pool):
            made = 0

            def const(ins):
                nonlocal made
                made += 1
                ins.then_inc(consts, 1)

            const(nc.gpsimd.memset(ident[:, :], 0.0))
            const(nc.gpsimd.memset(neg_ident[:, :], 0.0))
            pool.wait_ge(consts, 2)
            const(nc.gpsimd.affine_select(out=ident[:, :], in_=ident[:, :], compare_op=ALU.not_equal, fill=1.0,
                                          base=0, pattern=[[-1, P]], channel_multiplier=1))
            const(nc.gpsimd.affine_select(out=neg_ident[:, :], in_=neg_ident[:, :], compare_op=ALU.not_equal,
                                          fill=-BIG, base=0, pattern=[[-1, P]], channel_multiplier=1))
            const(nc.gpsimd.memset(ones_f[:, :], 1.0))
            const(nc.gpsimd.memset(ones_b[:, :], 1.0))
            const(nc.gpsimd.memset(zeros_b[:, :], 0.0))
            const(nc.gpsimd.memset(q_rows[:, :], 0.0))
            const(nc.gpsimd.memset(v_blk[:, :, :, :], 1.0))
            const(nc.gpsimd.iota(blk_idx[:, :], pattern=[[1, NB]], base=-(NB - 1), channel_multiplier=0))
            const(nc.gpsimd.iota(e_rank[:, :], pattern=[[-1, ER]], base=ER, channel_multiplier=0))
            const(nc.gpsimd.memset(k_ring[:, :, :, :], -1.0))
            pool.wait_ge(consts, N_CONST - 1)
            const(nc.gpsimd.memset(q_rows[0:1, :], 1.0))
            assert made == N_CONST
            pool.wait_ge(consts, N_CONST)
            for h in range(2):
                r0 = h * HALF + MASK_ROW
                pool.dma_start(q_st[r0:r0 + 1 + PARTS, :, :],
                               q_rows[:, :].unsqueeze(1).to_broadcast([1 + PARTS, NP, S])).then_inc(q_rows_in, 16)

            pool.wait_ge(csum_done, 1)
            pool.wait_ge(ctl_ready, 1)
            first = pool.value_load(ctl[0:1, 0:1], min_val=0, max_val=NB - 1)
            mixed = pool.value_load(ctl[0:1, 1:2], min_val=0, max_val=1)
            nblk = pool.value_load(ctl[0:1, 2:3], min_val=1, max_val=NB)
            with pool.Fori(0, nblk) as it:
                blk = block_of(it, first)
                pool.wait_ge(v_mm, it + 1)
                nc.gpsimd.tensor_copy(ctx_blk[:, :], ctx_all[:, bass.ds(blk * BLK, BLK)]).then_inc(ctx_copied, 1)
            pool.wait_ge(k_stored, nblk * (16 * len(K_TERM)))
            pool.wait_ge(v_stored, nblk * 16 + 16)
            pool.wait_ge(mrow_stored, 16)
            pool.sem_inc(tile_done, 2)

            for L in range(STAGES):
                with pool.If(mixed > 0):
                    with pool.Fori(0, nblk) as it:
                        blk = block_of(it, first)
                        g2 = pool.snap((it + nblk * L) * 2)
                        for b in range(2):
                            pool.wait_ge(tile_done, g2 + (b + 1))
                            nc.gpsimd.tensor_copy(m_ring[:, b, :, :],
                                                  mask_sb[:, :, bass.ds(blk * BLK + b * KT, KT)]) \
                                .then_inc(mask_tile, 1)
                if L < NP:
                    pool.wait_ge(max_split, 5 * (L + 1))
                    for b in range(4):
                        pool.dma_start(m_scr[L, :, :, 32 * b:32 * b + 32].rearrange("j c q -> c j q"),
                                       max_p[32 * b:32 * b + 2 * QT, :, :]).then_inc(max_stored, 16)
                    pool.wait_ge(max_stored, 64 * (L + 1))
                    for h in range(2):
                        r0 = h * HALF + MAX_ROW
                        pool.dma_start(q_st[r0:r0 + PARTS, L, :],
                                       m_scr[L, :, h * QT:(h + 1) * QT, :].rearrange("j t q -> j (t q)")) \
                            .then_inc(max_in, 16)

        @block.scalar
        def _(act):
            for dst, src in ((wq_sb[:, :], wqT), (bq_sb[:, :], bq), (wk_sb[:, :], wkT), (bk_sb[:, :], bk),
                             (wv_sb[:, :], wvT), (wo_sb[:, :], woT), (wr_sb[:, :], wrT),
                             (bv_sb[:, :], bv.to_broadcast([P, D])), (bo_sb[:, :], bo.to_broadcast([P, D])),
                             (rb_sb[:, :], rb.to_broadcast([P, ER]))):
                act.dma_start(dst, src).then_inc(small_in, 16)
            act.sem_inc(exp_done, 2)
            act.sem_inc(v_evac, 1)
            done = 0

            def step(ins):
                nonlocal done
                done += 1
                ins.then_inc(act_step, 1)

            def std_dev(v_at):
                act.wait_ge(dve_step, v_at)
                step(nc.scalar.activation(st8[:, 3, :], st8[:, 2, :], ACT.Sqrt))

            std_dev(V_XN1 - 2)
            for c in range(QC):
                act.wait_ge(pe_step, c + 1)
                step(nc.scalar.activation(xnT[:, c * 512:(c + 1) * 512], PS[:, c, :], ACT.Copy))
            act.wait_ge(ctx_in, 16)
            nc.scalar.activation(ctx_all[:, :], ctx_all[:, :], ACT.Copy, accum_out=csum[:, :]).then_inc(csum_done, 1)
            act.wait_ge(dve_step, V_AND)
            act.wait_ge(q_stored, 16)
            step(nc.scalar.activation(flags_bf[:, 0, :], mask_and[:, :].bitcast(U8), ACT.Copy))

            act.wait_ge(ctl_ready, 1)
            nblk = act.value_load(ctl[0:1, 2:3], min_val=1, max_val=NB)
            act.wait_ge(consts, N_CONST)
            with act.Fori(0, nblk) as it:
                act.wait_ge(v_mm, it + 2)
                act.wait_ge(v_stored, it * 16 + 16)
                nc.scalar.activation(v_blk[:, :, :, 0:HW],
                                     PS[:, 1, 0:2 * D].rearrange("p (t h w) -> p t h w", t=2, w=HW),
                                     ACT.Copy).then_inc(v_evac, 1)

            for L in range(2, STAGES):
                s = L - 2
                with act.Fori(0, nblk) as it:
                    g = act.snap(it + nblk * L)
                    e4 = act.snap((it + nblk * s) * 4)
                    for b in range(2):
                        act.wait_ge(tile_done, g * 2 + (b + 1))
                        for h in range(2):
                            act.wait_ge(sc_ready, e4 + (2 * b + h + 1))
                            nc.scalar.activation(prob[:, b, h, :],
                                                 PS[:, 2 * h:2 * h + 2, :].rearrange("p c q -> p (c q)"),
                                                 ACT.Exp).then_inc(exp_done, 1)
                act.wait_ge(tile_done, nblk * (2 * (L + 1)) + 2)
                nc.scalar.activation(o_sb[:, s, :], PS[:, OB + s % 2, :], ACT.Copy).then_inc(o_evac, 1)

            act.wait_ge(pe_step, 17)
            step(nc.scalar.activation(xnT[:, 0:512], PS[:, 0, :], ACT.Copy))
            std_dev(V_XN2 - 2)
            act.wait_ge(pe_step, 20)
            step(nc.scalar.activation(xnT[:, 0:512], PS[:, 0, :], ACT.Copy))
            act.wait_ge(dve_step, V_GAP)
            step(nc.scalar.activation(rs[:, 3, :], rs[:, 2, :], ACT.Exp))
            assert done == 8, done

            with act.Fori(0, E // 2) as i:
                for b in range(2):
                    for c in range(QC):
                        for ic, (_, n) in enumerate(ICH):
                            k = 6 * b + 3 * c + ic
                            act.wait_ge(gu_ready, i * 12 + (k + 1))
                            nc.scalar.activation(sg[0:n, k % 2, :], PS[0:n, k % 2, :], ACT.Silu) \
                                .then_inc(silu_done, 1)

        @block.tensor
        def _(pe):
            done = 0

            def step(ins):
                nonlocal done
                done += 1
                ins.then_inc(pe_step, 1)

            def transpose_tiles(src, c, bank):
                for j in range(4):
                    last = nc.tensor.transpose(PS[:, bank, j * P:(j + 1) * P], src[:, 4 * c + j, :], ident[:, :])
                step(last)

            pe.sem_inc(y_ready, 2)
            pe.sem_inc(v_mm, 1)
            pe.wait_ge(consts, N_CONST)
            pe.wait_ge(dve_step, V_XN1)
            for c in range(QC):
                transpose_tiles(tmp_b, c, c)
            pe.wait_ge(small_in, 16 * N_SMALL)
            for c in range(QC):
                pe.wait_ge(act_step, 2 + c)
                step(nc.tensor.matmul(PS[:, 2 + c, :], wq_sb[:, :], xnT[:, c * 512:(c + 1) * 512],
                                      start=True, stop=True))

            pe.wait_ge(act_step, 4)
            pe.wait_ge(dve_step, V_OR)
            with pe.Fori(0, NT) as t:
                for a in range(2):
                    nc.tensor.matmul(PS[:, 4, bass.ds(t + a * NT, 1)], flags_bf[:, a, bass.ds(t * KT, KT)],
                                     ones_b[:, :], start=True, stop=True)
            pe.drain().then_inc(pe_step, 1)
            done += 1
            pe.wait_ge(dve_step, V_FLAG)
            step(nc.tensor.transpose(PS[0:NT, 6, 0:P], flag[:, 0, :], ident[:, :]))
            step(nc.tensor.matmul(PS[0:1, 5, 0:2 * NT], ones_f[:, :], flag[:, 1:3, :].rearrange("p a t -> p (a t)"),
                                  start=True, stop=True))

            pe.wait_ge(ctl_ready, 1)
            mixed = pe.value_load(ctl[0:1, 1:2], min_val=0, max_val=1)
            nblk = pe.value_load(ctl[0:1, 2:3], min_val=1, max_val=NB)
            with pe.Fori(0, nblk) as it:
                pe.wait_ge(ctx_copied, it + 1)
                pe.wait_ge(k_split, it * 5 + 5)
                nc.tensor.matmul(PS[:, 0, 0:BLK], wk_sb[:, :], ctx_blk[:, :], start=True, stop=True) \
                    .then_inc(k_mm, 1)
                pe.wait_ge(v_evac, it + 1)
                for t in range(2):
                    last = nc.tensor.matmul(PS[:, 1, t * D:(t + 1) * D], ctx_blk[:, t * KT:(t + 1) * KT],
                                            wv_sb[:, :], start=True, stop=True)
                last.then_inc(v_mm, 1)

            pe.wait_ge(k_split, nblk * 5 + 5)
            pe.wait_ge(v_evac, nblk + 1)
            pe.wait_ge(q_stacked, 16 * 2 * len(Q_TERM))
            pe.wait_ge(q_rows_in, 32)

            def attention_blocks(L, masked):
                _, exp_at, max_at = pair_slice(L)
                s = L - 2

                def head_scores(e4, b):
                    for h in range(2):
                        pe.wait_ge(exp_done, e4 + (2 * b + h + 1))
                        r = slice(h * HALF, h * HALF + ROWS)
                        for c in range(QC):
                            last = nc.tensor.matmul(PS[:, 2 * h + c, :], k_ring[r, b, exp_at, :],
                                                    q_st[r, s, c * 512:(c + 1) * 512],
                                                    start=True, stop=not masked)
                            if masked:
                                for j in range(4):
                                    last = nc.tensor.matmul(PS[:, 2 * h + c, j * P:(j + 1) * P],
                                                            m_ring[:, b, 4 * c + j, :], neg_ident[:, :],
                                                            start=False, stop=j == 3)
                        last.then_inc(sc_ready, 1)

                def max_units(u8, b, ends_tile):
                    for u in range(4):
                        g, h = divmod(u, 2)
                        pe.wait_ge(max_done, u8 + (4 * b + u + 1))
                        r = slice(h * HALF, h * HALF + ROWS)
                        for j in range(4):
                            t = 4 * g + j
                            last = nc.tensor.matmul(PS[:, SM + u % 2, j * KT:(j + 1) * KT],
                                                    q_st[r, L, t * P:(t + 1) * P], k_ring[r, b, max_at, :],
                                                    start=True, stop=not masked)
                            if masked:
                                last = nc.tensor.matmul(PS[:, SM + u % 2, j * KT:(j + 1) * KT],
                                                        neg_ident[:, :], m_ring[:, b, t, :],
                                                        start=False, stop=True)
                        last.then_inc(sm_ready, 1)
                    if ends_tile:
                        pe.wait_ge(sm_ready, u8 + (4 * b + 4))
                        pe.sem_inc(tile_done, 1)

                def weighted_values(e4, b):
                    pe.wait_ge(exp_done, e4 + (2 * b + 2 + 2))
                    for g in range(4):
                        h, c = divmod(g, 2)
                        last = nc.tensor.matmul(PS[32 * g:32 * g + HW + 1, OB + s % 2, :],
                                                v_ring[:, b, h * (HW + 1):(h + 1) * (HW + 1)],
                                                prob[:, b, h, c * 512:(c + 1) * 512],
                                                start=False, stop=True, skip_group_check=True)
                    last.then_inc(tile_done, 1)

                with pe.Fori(0, nblk) as it:
                    g = pe.snap(it + nblk * L)
                    u8 = pe.snap(g * 8)
                    if exp_at is not None:
                        e4 = pe.snap((it + nblk * s) * 4)
                    for b in range(2):
                        pe.wait_ge(ring_in[b], g * 48 + 48)
                        if masked:
                            pe.wait_ge(mask_tile, g * 2 + (b + 1))
                        if exp_at is not None:
                            head_scores(e4, b)
                            if b == 1:
                                weighted_values(e4, 0)
                        if max_at is not None:
                            max_units(u8, b, exp_at is None)
                    if exp_at is not None:
                        weighted_values(e4, 1)

            for L in range(STAGES):
                if L >= 2:
                    s = L - 2
                    pe.wait_ge(max_in, 32 * (s + 1))
                    if s >= 2:
                        pe.wait_ge(o_evac, s - 1)
                    nc.tensor.matmul(PS[:, OB + s % 2, :], zeros_b[:, 0:P], zeros_b[:, :], start=True, stop=True,
                                     skip_group_check=True)
                with pe.If(mixed > 0):
                    attention_blocks(L, True)
                with pe.Else():
                    attention_blocks(L, False)

            pe.wait_ge(o_evac, NP)
            for s in range(NP):
                transpose_tiles(o_sb[:, s, :].rearrange("p (j q) -> p j q", j=4), 0, s)
            pe.wait_ge(dve_step, V_NORM)
            step(nc.tensor.matmul(PS[:, 0, 0:P], csum_b[:, :], wv_sb[:, :], start=True, stop=True))
            pe.wait_ge(dve_step, V_ATT)
            for c in range(QC):
                transpose_tiles(tmp_a, c, c)
            pe.wait_ge(act_step, 5)
            pe.wait_ge(dve_step, V_ATT_T)
            for t in range(QT):
                last = nc.tensor.matmul(PS[:, 2 + t // 4, (t % 4) * P:(t % 4 + 1) * P], xnT[:, t * P:(t + 1) * P],
                                        wo_sb[:, :], start=True, stop=True)
            step(last)
            pe.wait_ge(dve_step, V_XN2)
            for c in range(QC):
                transpose_tiles(tmp_b, c, c)
            pe.wait_ge(act_step, 7)
            pe.wait_ge(dve_step, V_XN2_T)
            for t in range(QT):
                last = nc.tensor.matmul(PS[:, 6, t * ER:(t + 1) * ER], xnT[:, t * P:(t + 1) * P], wr_sb[:, :],
                                        start=True, stop=True)
            step(last)
            assert done == 22, done

            def gate_up(i, b, c):
                for ic, (o, n) in enumerate(ICH):
                    k = 6 * b + 3 * c + ic
                    pe.wait_ge(hid_done, i * 12 + (k + 1))
                    for a in range(2):
                        last = nc.tensor.matmul(PS[0:n, 2 * a + k % 2, :],
                                                w_gu[:, b, a * I + o:a * I + o + n],
                                                xnT[:, c * 512:(c + 1) * 512], start=True, stop=True)
                    last.then_inc(gu_ready, 1)

            def down(i, b, c):
                pe.wait_ge(hid_done, i * 12 + (6 * b + 3 * c + 3 + 2))
                pe.wait_ge(y_used, i * 4 + (2 * b + c + 1))
                for t in range(4):
                    for ic, (_, n) in enumerate(ICH):
                        last = nc.tensor.matmul(PS[:, 4 + c, t * P:(t + 1) * P],
                                                hid[0:n, c, ic, t * P:(t + 1) * P], w_dn[0:n, b, ic, :],
                                                start=ic == 0, stop=ic == NI - 1)
                last.then_inc(y_ready, 1)

            with pe.Fori(0, E // 2) as i:
                pe.wait_ge(w_in[0], i * 48 + 48)
                gate_up(i, 0, 0)
                gate_up(i, 0, 1)
                down(i, 0, 0)
                pe.wait_ge(w_in[1], i * 48 + 48)
                gate_up(i, 1, 0)
                down(i, 0, 1)
                gate_up(i, 1, 1)
                down(i, 1, 0)
                down(i, 1, 1)

        @block.vector
        def _(dve):
            done = 0

            def step(ins, wait=True):
                nonlocal done
                done += 1
                ins.then_inc(dve_step, 1)
                if wait:
                    dve.wait_ge(dve_step, done)

            def per_tile(v):
                return v.unsqueeze(2).to_broadcast([P, QT, D])

            def mark(value):
                assert done == value, (done, value)

            def layernorm(src, root):
                step(nc.vector.tensor_reduce(st8[:, 0, :], src[:, :, :], AX, ALU.add))
                step(nc.vector.tensor_scalar(st8[:, 1, :], st8[:, 0, :], -1.0 / D, None, ALU.mult))
                step(nc.vector.tensor_tensor(tmp_b[:, :, :], src[:, :, :], per_tile(st8[:, 1, :]), ALU.add))
                step(nc.vector.tensor_tensor(tmp_a[:, :, :], tmp_b[:, :, :], tmp_b[:, :, :], ALU.mult))
                step(nc.vector.tensor_reduce(st8[:, 0, :], tmp_a[:, :, :], AX, ALU.add))
                step(nc.vector.tensor_scalar(st8[:, 2, :], st8[:, 0, :], 1.0 / D, 1e-5, ALU.mult, ALU.add))
                dve.wait_ge(act_step, root)
                step(nc.vector.reciprocal(st8[:, 4, :], st8[:, 3, :]))
                step(nc.vector.tensor_tensor(tmp_b[:, :, :], tmp_b[:, :, :], per_tile(st8[:, 4, :]), ALU.mult))

            dve.sem_inc(k_split, 5)
            dve.wait_ge(x_in, 16)
            layernorm(x_sb, 1)
            mark(V_XN1)

            dve.wait_ge(small_in, 16 * N_SMALL)
            dve.wait_ge(pe_step, 4)
            q32 = tmp_b[:, :, :].rearrange("p t d -> p (t d)")
            rest = tmp_a[:, :, :].rearrange("p t d -> p (t d)")
            step(nc.vector.tensor_scalar(q32, PS[:, 2:4, :].rearrange("p c q -> p (c q)"), bq_sb[:, :], None, ALU.add))
            step(nc.vector.tensor_copy(q_parts[:, 0, :], q32))
            step(nc.vector.tensor_tensor(rest, q32, q_parts[:, 0, :], ALU.subtract))
            step(nc.vector.tensor_copy(q_parts[:, 1, :], rest))
            step(nc.vector.tensor_tensor(q_parts[:, 2, :], rest, q_parts[:, 1, :], ALU.subtract))
            mark(V_QPARTS)

            words = [mask_sb[:, t, :].bitcast(I32) for t in range(QT)]
            dve.wait_ge(mask_in[0], 16)
            for t in range(1, QT):
                dve.wait_ge(mask_in[t], 16)
                step(nc.vector.tensor_tensor(mask_and[:, :], words[0] if t == 1 else mask_and[:, :], words[t],
                                             ALU.bitwise_and))
                if t == QT - 1:
                    mark(V_AND)
                step(nc.vector.tensor_tensor(mask_or[:, :], words[0] if t == 1 else mask_or[:, :], words[t],
                                             ALU.bitwise_or))
            step(nc.vector.tensor_copy(flags_bf[:, 1, :], mask_or[:, :].bitcast(U8)))
            mark(V_OR)

            dve.wait_ge(pe_step, 5)
            step(nc.vector.tensor_scalar(flag[:, 0, :], PS[:, 4, 0:NT], P - 0.5, None, ALU.is_ge))
            step(nc.vector.tensor_scalar(flag[:, 1, :], flag[:, 0, :], -1.0, 1.0, ALU.mult, ALU.add))
            step(nc.vector.scalar_tensor_tensor(flag[:, 2, :], PS[:, 4, NT:2 * NT], 0.5, flag[:, 0, :],
                                                ALU.is_ge, ALU.subtract))
            mark(V_FLAG)
            dve.wait_ge(pe_step, 7)
            step(nc.vector.tensor_scalar(mrow_bf[:, :], PS[0:NT, 6, 0:KT], -BIG, None, ALU.mult))
            mark(V_MROW)
            dve.wait_ge(consts, N_CONST)
            step(nc.vector.tensor_reduce(row[:, 0, :], PS[0:1, 5, 0:2 * NT].rearrange("p (n t) -> p n t", t=2),
                                         AX, ALU.max))
            step(nc.vector.tensor_copy(blk_idx_f[:, :], blk_idx[:, :]))
            step(nc.vector.scalar_tensor_tensor(row[:, 1, 0:NB], row[:, 0, 0:NB], 0.5, blk_idx_f[:, :],
                                                ALU.is_ge, ALU.mult))
            step(nc.vector.tensor_reduce(row[:, 2, 0:1], row[:, 1, 0:NB], AX, ALU.min))
            step(nc.vector.tensor_scalar(ctl[:, 0:1], row[:, 2, 0:1], float(NB - 1), None, ALU.add))
            step(nc.vector.tensor_reduce(row[:, 3, 0:1], row[:, 0, NB:2 * NB], AX, ALU.max))
            step(nc.vector.tensor_scalar(ctl[:, 2:3], row[:, 2, 0:1], -1.0, 1.0, ALU.mult, ALU.add))
            nc.vector.tensor_scalar(ctl[:, 1:2], row[:, 3, 0:1], 0.5, None, ALU.is_ge).then_inc(ctl_ready, 1)

            step(nc.vector.tensor_tensor(acc[:, :, :], x_sb[:, :, :],
                                         bo_sb[:, :].unsqueeze(1).to_broadcast([P, QT, D]), ALU.add))
            step(nc.vector.tensor_copy(e_rank_f[:, :], e_rank[:, :]))
            dve.wait_ge(csum_done, 1)
            step(nc.vector.tensor_copy(csum_b[:, :], csum[:, :].to_broadcast([P, P])))
            mark(V_CSUM)

            dve.wait_ge(ctl_ready, 1)
            first = dve.value_load(ctl[0:1, 0:1], min_val=0, max_val=NB - 1)
            nblk = dve.value_load(ctl[0:1, 2:3], min_val=1, max_val=NB)
            with dve.Fori(0, nblk) as it:
                blk = block_of(it, first)
                it5 = dve.snap(it * 5 + 5)
                cols = bass.ds(blk * BLK, BLK)
                dve.wait_ge(k_mm, it + 1)
                nc.vector.tensor_scalar(k32[:, :], PS[:, 0, 0:BLK], bk_sb[:, :], None, ALU.add).then_inc(k_split, 1)
                dve.wait_ge(k_split, it5 + 1)
                nc.vector.tensor_copy(k_parts[:, 0, cols], k32[:, :]).then_inc(k_split, 1)
                dve.wait_ge(k_split, it5 + 2)
                nc.vector.tensor_tensor(kr1[:, :], k32[:, :], k_parts[:, 0, cols], ALU.subtract).then_inc(k_split, 1)
                dve.wait_ge(k_split, it5 + 3)
                nc.vector.tensor_copy(k_parts[:, 1, cols], kr1[:, :]).then_inc(k_split, 1)
                dve.wait_ge(k_split, it5 + 4)
                nc.vector.tensor_tensor(k_parts[:, 2, cols], kr1[:, :], k_parts[:, 1, cols], ALU.subtract) \
                    .then_inc(k_split, 1)

            nc.vector.memset(maxT[:, :], 0.0).then_inc(max_init, 1)
            nc.vector.memset(run_max[:, :], FLOOR).then_inc(max_init, 1)
            dve.sem_inc(max_done, 2)
            dve.sem_inc(max_fold, 2)
            for L in range(NP):
                if L:
                    nc.vector.memset(run_max[:, 0:2 * QT], FLOOR).then_inc(max_init, 1)
                dve.wait_ge(max_init, 2 + L)
                with dve.Fori(0, nblk) as it:
                    g = dve.snap(it + nblk * L)
                    u8 = dve.snap(g * 8)
                    dve.wait_ge(max_fold, g * 2 + 2)
                    for b in range(2):
                        for u in range(4):
                            qg, h = divmod(u, 2)
                            dve.wait_ge(sm_ready, u8 + (4 * b + u + 1))
                            n0 = h * QT + 4 * qg
                            nc.vector.tensor_reduce(tile_max[:, b, n0:n0 + 4],
                                                    PS[:, SM + u % 2, :].rearrange("p (t k) -> p t k", k=KT),
                                                    AX, ALU.max).then_inc(max_done, 1)
                    dve.wait_ge(max_done, u8 + 8 + 2)
                    nc.vector.tensor_tensor(tile_max[:, 0, :], tile_max[:, 0, :], tile_max[:, 1, :], ALU.max) \
                        .then_inc(max_fold, 1)
                    dve.wait_ge(max_fold, g * 2 + (1 + 2))
                    nc.vector.tensor_tensor(run_max[:, 0:2 * QT], run_max[:, 0:2 * QT], tile_max[:, 0, :], ALU.max) \
                        .then_inc(max_fold, 1)
                dve.wait_ge(max_fold, nblk * (2 * (L + 1)) + 2)
                nc.vector.transpose(maxT[:, :], run_max[:, :]).then_inc(max_split, 1)
                dve.wait_ge(max_split, 5 * L + 1)
                if L:
                    dve.wait_ge(max_stored, 64 * L)
                nc.vector.tensor_copy(max_p[:, 0, :], maxT[:, :]).then_inc(max_split, 1)
                dve.wait_ge(max_split, 5 * L + 2)
                nc.vector.tensor_tensor(max_r[:, :], maxT[:, :], max_p[:, 0, :], ALU.subtract).then_inc(max_split, 1)
                dve.wait_ge(max_split, 5 * L + 3)
                nc.vector.tensor_copy(max_p[:, 1, :], max_r[:, :]).then_inc(max_split, 1)
                dve.wait_ge(max_split, 5 * L + 4)
                nc.vector.tensor_tensor(max_p[:, 2, :], max_r[:, :], max_p[:, 1, :], ALU.subtract) \
                    .then_inc(max_split, 1)

            dve.wait_ge(pe_step, 15)
            o_t = PS[:, :, :].rearrange("p s (n r) -> p (s n) r", r=32)
            step(nc.vector.tensor_scalar(none_l[:, :], o_t[:, :, HW], 0.0, None, ALU.is_equal))
            step(nc.vector.tensor_tensor(den[:, :], o_t[:, :, HW], none_l[:, :], ALU.add))
            step(nc.vector.reciprocal(den[:, :], den[:, :]))

            def heads_of(v, h, c):
                return v[:, 4 * c:4 * c + 4, :].rearrange("p j (s h w) -> p s j h w", h=2, w=HW)[:, :, :, h, :]

            def of_group(v, h, c):
                return v[:, :].rearrange("p (s j g) -> p s j g", s=NP, g=4)[:, :, :, 2 * h + c] \
                    .unsqueeze(3).to_broadcast([P, NP, 4, HW])

            for h in range(2):
                for c in range(QC):
                    step(nc.vector.tensor_tensor(
                        heads_of(tmp_a, h, c),
                        PS[:, :, :].rearrange("p s (j g r) -> p s j g r", j=4, r=32)[:, :, :, 2 * h + c, 0:HW],
                        of_group(den, h, c), ALU.mult))
            mark(V_NORM)
            dve.wait_ge(pe_step, 16)
            step(nc.vector.tensor_scalar(csum_b[:, :], PS[:, 0, 0:D], 1.0 / T, None, ALU.mult))
            for h in range(2):
                for c in range(QC):
                    step(nc.vector.tensor_tensor(
                        heads_of(tmp_b, h, c), of_group(none_l, h, c),
                        csum_b[:, :].rearrange("p (s h w) -> p s h w", h=2, w=HW)[:, :, h, :]
                        .unsqueeze(2).to_broadcast([P, NP, 4, HW]), ALU.mult))
            step(nc.vector.tensor_tensor(tmp_a[:, :, :], tmp_a[:, :, :], tmp_b[:, :, :], ALU.add))
            step(nc.vector.tensor_tensor(tmp_a[:, :, :], tmp_a[:, :, :],
                                         bv_sb[:, :].unsqueeze(1).to_broadcast([P, QT, D]), ALU.add))
            mark(V_ATT)
            dve.wait_ge(pe_step, 18)
            step(nc.vector.tensor_copy(xnT[:, 512:1024], PS[:, 1, :]))
            mark(V_ATT_T)
            dve.wait_ge(pe_step, 19)
            flat = acc[:, :, :].rearrange("p t d -> p (t d)")
            step(nc.vector.scalar_tensor_tensor(flat, PS[:, 2:4, :].rearrange("p c q -> p (c q)"),
                                                float(HW) ** -0.5, flat, ALU.mult, ALU.add))
            layernorm(acc, 6)
            mark(V_XN2)
            dve.wait_ge(pe_step, 21)
            step(nc.vector.tensor_copy(xnT[:, 512:1024], PS[:, 1, :]))
            mark(V_XN2_T)

            def per_expert(v):
                return v.unsqueeze(2).to_broadcast([P, QT, ER])

            rank = e_rank_f[:, :].unsqueeze(1).to_broadcast([P, QT, ER])

            def pick(logits, top, hot, tmp):
                step(nc.vector.tensor_reduce(top, logits, AX, ALU.max))
                step(nc.vector.tensor_tensor(hot, logits, per_expert(top), ALU.is_equal))
                step(nc.vector.tensor_tensor(tmp, hot, rank, ALU.mult))
                step(nc.vector.tensor_reduce(rs[:, 1, :], tmp, AX, ALU.max))
                step(nc.vector.tensor_tensor(hot, tmp, per_expert(rs[:, 1, :]), ALU.is_equal))

            dve.wait_ge(pe_step, 22)
            step(nc.vector.tensor_tensor(rt[:, 0, :, :], PS[:, 6, 0:QT * ER].rearrange("p (t e) -> p t e", e=ER),
                                         rb_sb[:, :].unsqueeze(1).to_broadcast([P, QT, ER]), ALU.add))
            pick(rt[:, 0, :, :], rs[:, 0, :], rt[:, 1, :, :], rt[:, 2, :, :])
            step(nc.vector.scalar_tensor_tensor(rt[:, 2, :, :], rt[:, 1, :, :], -BIG, rt[:, 0, :, :],
                                                ALU.mult, ALU.add))
            pick(rt[:, 2, :, :], rs[:, 4, :], rt[:, 3, :, :], rt[:, 4, :, :])
            step(nc.vector.tensor_tensor(rs[:, 2, :], rs[:, 4, :], rs[:, 0, :], ALU.subtract))
            mark(V_GAP)
            dve.wait_ge(act_step, 8)
            step(nc.vector.tensor_scalar(rs[:, 1, :], rs[:, 3, :], 1.0, None, ALU.add))
            step(nc.vector.reciprocal(rs[:, 1, :], rs[:, 1, :]))
            step(nc.vector.tensor_tensor(rs[:, 5, :], rs[:, 3, :], rs[:, 1, :], ALU.mult))
            step(nc.vector.tensor_tensor(rt[:, 1, :, :], rt[:, 1, :, :], per_expert(rs[:, 1, :]), ALU.mult))
            step(nc.vector.tensor_tensor(rt[:, 3, :, :], rt[:, 3, :, :], per_expert(rs[:, 5, :]), ALU.mult))
            step(nc.vector.tensor_tensor(w_all[:, 1:E, :], rt[:, 1, :, :].rearrange("p t e -> p e t"),
                                         rt[:, 3, :, :].rearrange("p t e -> p e t"), ALU.add))
            step(nc.vector.memset(w_all[:, 0, :], 1.0))

            dve.sem_inc(hid_done, 2)
            dve.sem_inc(y_used, 2)
            with dve.Fori(0, E // 2) as i:
                dve.wait_ge(y_used, i * 4 + 2)
                nc.vector.tensor_copy(w_cur[:, :, :], w_all[:, bass.ds(i * 2, 2), :]).then_inc(w_copied, 1)

                def hidden(b, c):
                    dve.wait_ge(y_ready, i * 4 + (2 * b + c + 1))
                    for ic, (_, n) in enumerate(ICH):
                        k = 6 * b + 3 * c + ic
                        dve.wait_ge(silu_done, i * 12 + (k + 1))
                        nc.vector.tensor_tensor(hid[0:n, c, ic, :], sg[0:n, k % 2, :], PS[0:n, 2 + k % 2, :],
                                                ALU.mult).then_inc(hid_done, 1)

                def add_output(b, c):
                    dve.wait_ge(y_ready, i * 4 + (2 * b + c + 1 + 2))
                    dve.wait_ge(y_used, i * 4 + (2 * b + c + 1))
                    for t in range(4):
                        tile = acc[:, 4 * c + t, :]
                        last = nc.vector.scalar_tensor_tensor(tile, PS[:, 4 + c, t * P:(t + 1) * P],
                                                              w_cur[:, b, 4 * c + t:4 * c + t + 1], tile,
                                                              ALU.mult, ALU.add)
                    last.then_inc(y_used, 1)

                hidden(0, 0)
                hidden(0, 1)
                dve.wait_ge(w_copied, i + 1)
                add_output(0, 0)
                hidden(1, 0)
                add_output(0, 1)
                hidden(1, 1)
                add_output(1, 0)
                add_output(1, 1)


def kernel(**inputs):
    import numpy as np
    import concourse.bacc as bacc
    from concourse.bass_utils import run_bass_kernel_spmd as run

    a = {n: np.asarray(v) for n, v in inputs.items()}
    at, ff = "L0_xattn_", "L0_ffn_"
    x = a["x"][0]
    S, D = x.shape
    T = a["ctx_1024"].shape[1]
    front = padded_keys(T) - T
    I = a[ff + "sg"].shape[0]
    g = np.concatenate([a[ff + "sg"][None], a[ff + "rg"]]).transpose(0, 2, 1)
    u = np.concatenate([a[ff + "su"][None], a[ff + "ru"]]).transpose(0, 2, 1)
    arrays = {
        "x": x,
        "ctxT": np.pad(a["ctx_1024"][0].T, ((0, 0), (front, 0))),
        "mask": np.pad(a["mask_SxS2_bk1"], ((0, 0), (front, 0)), constant_values=True),
        "wqT": a[at + "Wq"].reshape(D, D).T, "bq": a[at + "bq"].reshape(D, 1),
        "wkT": a[at + "Wk"].reshape(D, D).T, "bk": a[at + "bk"].reshape(D, 1),
        "wvT": a[at + "Wv"].reshape(D, D).T, "bv": a[at + "bv"].reshape(1, D),
        "woT": a[at + "Wo"].reshape(D, D).T, "bo": a[at + "bo"].reshape(1, D),
        "gu": np.concatenate([g, u], axis=2),
        "dn": np.concatenate([a[ff + "sd"][None], a[ff + "rd"]]).transpose(0, 2, 1),
        "wrT": a[ff + "wr"].T, "rb": a[ff + "rb"].reshape(1, -1),
    }
    arrays = {n: np.ascontiguousarray(v) for n, v in arrays.items()}
    nc = bacc.Bacc("TRN2", target_bir_lowering=False, num_devices=1)
    args = {n: nc.dram_tensor(f"in_{n}", v.shape, mybir.dt.from_np(v.dtype), kind="ExternalInput").ap()
            for n, v in arrays.items()}
    out = nc.dram_tensor("out", (1, S, D), F32, kind="ExternalOutput").ap()
    xattn_moe(nc, *args.values(), out, T)
    r = run(nc, [{f"in_{n}": v for n, v in arrays.items()}], core_ids=[0])
    return r.results[0]["out"]
```

```python
from contextlib import ExitStack

import concourse.bass as bass
from concourse import mybir

F32 = mybir.dt.float32
BF16 = mybir.dt.bfloat16
I32 = mybir.dt.int32
U8 = mybir.dt.uint8
ALU = mybir.AluOpType
ACT = mybir.ActivationFunctionType
AX = mybir.AxisListType.X

P = 128
KT = 128
BLK = 2 * KT
HW = 8
PARTS = 3
K_ROW = (0, 3 * HW, 5 * HW)
MASK_ROW = 6 * HW
MAX_ROW = MASK_ROW + 1
HALF = 64
BIG = float(2.0 ** 100)
FLOOR = -1.0e9


def padded_keys(T):
    return -(-T // BLK) * BLK


def xattn_moe(nc, x, ctxT, mask, wqT, bq, wkT, bk, wvT, bv, woT, bo, gu, dn, wrT, rb, out, T):
    S, D = x.shape
    QT = S // P
    QC = S // 512
    TP = ctxT.shape[1]
    NB = TP // BLK
    NT = TP // KT
    H = D // HW
    NP = H // 2
    STAGES = NP + 2
    E, _, I2 = gu.shape
    I = I2 // 2
    ER = E - 1
    ICH = [(o, min(P, I - o)) for o in range(0, I, P)]
    NI = len(ICH)
    PIECES = [(t, min(8, NT - t)) for t in range(0, NT, 8)]
    MW = 8 * KT // 4
    assert D == P and QC == 2 and QT == 8 and H == 16 and NI == 3 and E % 2 == 0 and NB % 2 == 0

    k_scr = nc.dram_tensor("k_scr", (H, MAX_ROW, TP), BF16, kind="Internal").ap()
    v_scr = nc.dram_tensor("v_scr", (NT, KT, H * (HW + 1)), F32, kind="Internal").ap()
    q_scr = nc.dram_tensor("q_scr", (PARTS, D, S), BF16, kind="Internal").ap()
    m_scr = nc.dram_tensor("m_scr", (NP, PARTS, 2 * QT, P), BF16, kind="Internal").ap()

    with ExitStack() as ctx:
        def sb(name, shape, dt=F32):
            return ctx.enter_context(nc.sbuf_tensor(name, shape, dt))

        def sem(name):
            return ctx.enter_context(nc.semaphore(name))

        PS = ctx.enter_context(nc.psum_tensor("PS", [P, 8, 512], F32))
        SM = 2
        OB = 6

        x_sb = sb("x_sb", [P, QT, D])
        mask_sb = sb("mask_sb", [P, QT, TP], U8)
        mask_and = sb("mask_and", [P, TP // 4], I32)
        mask_or = sb("mask_or", [P, TP // 4], I32)
        flags_bf = sb("flags_bf", [P, 2, TP], BF16)
        o_sb = flags_bf[:, :, :].rearrange("p a k -> p (a k)")[:, 0:NP * 1024].bitcast(F32) \
            .rearrange("p (s q) -> p s q", s=NP)
        m_ring = mask_and[:, 0:QT * KT].bitcast(BF16).rearrange("p (b t k) -> p b t k", b=2, t=QT)
        acc = mask_or[:, 0:S].bitcast(F32).rearrange("p (t d) -> p t d", t=QT)
        ctx_all = sb("ctx_all", [P, TP])
        prob = ctx_all[:, 0:4096].rearrange("p (b v q) -> p b v q", b=2, v=2 * QC)
        k_parts = sb("k_parts", [P, PARTS, TP], BF16)
        late = k_parts[:, :, :].rearrange("p j k -> p (j k)").bitcast(F32)
        tree = [[late[:, o + n:o + n + w].bitcast(I32) for n, w in ((0, 4 * MW), (4 * MW, 2 * MW))]
                for o in (0, 6 * MW)]
        q_parts = late[:, 4096:4096 + PARTS * S // 2].bitcast(BF16).rearrange("p (j q) -> p j q", j=PARTS)
        sizes = (2 * NI * 512, 2 * 512, 2 * I2, 2 * NI * D, 6 * QT * ER, NP * 16, NP * 16)
        ends = [sum(sizes[:n + 1]) for n in range(len(sizes))]
        hid = late[:, 0:ends[0]].rearrange("p (c n q) -> p c n q", c=2, n=NI)
        sg = late[:, ends[0]:ends[1]].rearrange("p (b q) -> p b q", b=2)
        w_gu = late[:, ends[1]:ends[2]].rearrange("p (b i) -> p b i", b=2)
        w_dn = late[:, ends[2]:ends[3]].rearrange("p (b n o) -> p b n o", b=2, n=NI)
        rt = late[:, ends[3]:ends[4]].rearrange("p (n t e) -> p n t e", n=6, t=QT)
        none_l = late[:, ends[4]:ends[5]]
        den = late[:, ends[5]:ends[6]]
        q_st = sb("q_st", [P, NP, S], BF16)
        wq_sb = sb("wq_sb", [P, D])
        wk_sb = sb("wk_sb", [P, D])
        wv_sb = sb("wv_sb", [P, D])
        wo_sb = sb("wo_sb", [P, D])
        wr_sb = sb("wr_sb", [P, ER])
        bq_sb = sb("bq_sb", [P, 1])
        bk_sb = sb("bk_sb", [P, 1])
        bv_sb = sb("bv_sb", [P, D])
        bo_sb = sb("bo_sb", [P, D])
        rb_sb = sb("rb_sb", [P, ER])
        ident = sb("ident", [P, P])
        neg_ident = sb("neg_ident", [P, P], BF16)
        ones_f = sb("ones_f", [P, 1])
        ones_b = sb("ones_b", [P, 1], BF16)
        zeros_b = sb("zeros_b", [P, 512], BF16)
        q_rows = sb("q_rows", [1 + PARTS, S], BF16)
        blk_idx = sb("blk_idx", [1, NB], I32)
        blk_idx_f = sb("blk_idx_f", [1, NB])
        e_rank = sb("e_rank", [P, ER], I32)
        e_rank_f = sb("e_rank_f", [P, ER])
        tmp_a = sb("tmp_a", [P, QT, D])
        tmp_b = sb("tmp_b", [P, QT, D])
        xnT = sb("xnT", [P, S])
        st8 = sb("st8", [P, 6, QT])
        flag = sb("flag", [P, 3, NT])
        row = sb("row", [1, 4, 2 * NB])
        ctl = sb("ctl", [1, 3], I32)
        mrow_bf = sb("mrow_bf", [NT, KT], BF16)
        ctx_blk = sb("ctx_blk", [P, BLK])
        kr1 = sb("kr1", [P, BLK])
        v_blk = sb("v_blk", [P, 2, H, HW + 1])
        csum = sb("csum", [P, 1])
        csum_b = sb("csum_b", [P, P])
        k_ring = sb("k_ring", [P, 2, 2, 2, BLK], BF16)
        v_ring = sb("v_ring", [P, 2, 2 * (HW + 1)])
        tile_max = sb("tile_max", [P, 2, 2 * QT])
        run_max = sb("run_max", [P, 32])
        maxT = sb("maxT", [P, 32])
        max_r = sb("max_r", [P, 32])
        max_p = sb("max_p", [P, PARTS, 32], BF16)
        rs = sb("rs", [P, 6, QT])
        w_all = sb("w_all", [P, E, QT])
        w_cur = sb("w_cur", [P, 2, QT])

        x_in = sem("x_in")
        mask_in = [sem(f"mask_in{n}") for n in range(len(PIECES))]
        mask_tree = sem("mask_tree")
        mask_cast = sem("mask_cast")
        ctx_in = sem("ctx_in")
        q_weights = sem("q_weights")
        small_in = sem("small_in")
        consts = sem("consts")
        dve_step = sem("dve_step")
        act_step = sem("act_step")
        pe_step = sem("pe_step")
        csum_done = sem("csum_done")
        q_stored = sem("q_stored")
        q_stacked = sem("q_stacked")
        q_rows_in = sem("q_rows_in")
        mrow_stored = sem("mrow_stored")
        ctl_ready = sem("ctl_ready")
        ctx_copied = sem("ctx_copied")
        k_mm = sem("k_mm")
        v_mm = sem("v_mm")
        k_part0 = sem("k_part0")
        k_split = sem("k_split")
        v_evac = sem("v_evac")
        v_stored = sem("v_stored")
        k_stored = sem("k_stored")
        q_zeroed = sem("q_zeroed")
        k_in = sem("k_in")
        v_in = [sem("v_in0"), sem("v_in1")]
        tile_done = sem("tile_done")
        mask_tile = sem("mask_tile")
        sc_ready = sem("sc_ready")
        exp_done = sem("exp_done")
        sm_ready = sem("sm_ready")
        max_done = sem("max_done")
        max_init = sem("max_init")
        max_fold = sem("max_fold")
        max_split = sem("max_split")
        max_stored = sem("max_stored")
        max_in = sem("max_in")
        o_evac = sem("o_evac")
        w_in = [sem("w_in0"), sem("w_in1")]
        gu_ready = sem("gu_ready")
        silu_done = sem("silu_done")
        hid_done = sem("hid_done")
        w_copied = sem("w_copied")
        y_ready = sem("y_ready")
        y_used = sem("y_used")
        out_done = sem("out_done")

        N_CONST = 15
        N_SMALL = 8

        def pair_slice(L):
            if L < 2:
                return slice(L, L + 3, 2), None, 0
            if L < NP:
                return slice(L - 2, L + 1, 2), 0, 1
            return slice(L - 4, L - 1, 2), 1, None

        V_XN1 = 8
        V_QPARTS = 13
        V_FLAG = 16
        V_MROW = 17
        V_NORM = 34
        V_ATT = 41
        V_ATT_T = 42
        V_XN2 = 51
        V_XN2_T = 52
        V_GAP = 65

        def block_of(it, first):
            return nc.s_assert_within(it + first, 0, NB - 1, skip_runtime_bounds_check_because="it < NB - first")

        block = ctx.enter_context(nc.Block())

        @block.sync
        def _(sp):
            sp.sem_inc(v_stored, 16)
            sp.dma_start(x_sb[:, :, :], x.rearrange("(t p) d -> p t d", p=P)).then_inc(x_in, 16)
            sp.dma_start(wq_sb[:, :], wqT).then_inc(q_weights, 16)
            sp.dma_start(bq_sb[:, :], bq).then_inc(q_weights, 16)
            for n, (t0, nt) in enumerate(PIECES):
                cols = slice(t0 * KT, (t0 + nt) * KT)
                sp.dma_start(mask_sb[:, :, cols], mask.rearrange("(t p) k -> p t k", p=P)[:, :, cols]) \
                    .then_inc(mask_in[n], 16)
            sp.dma_start(ctx_all[:, :], ctxT).then_inc(ctx_in, 16)

            sp.wait_ge(dve_step, V_QPARTS)
            sp.dma_start(q_scr.rearrange("j r q -> r j q"), q_parts[:, :, :]).then_inc(q_stored, 16)
            sp.wait_ge(q_stored, 16)
            sp.wait_ge(q_zeroed, 2)
            q_src = q_scr.rearrange("j (p h w) q -> j h w p q", h=2, w=HW)
            for h in range(2):
                for j in range(PARTS):
                    n = PARTS - j
                    for i in range(n):
                        r0 = h * HALF + K_ROW[j] + i
                        sp.dma_start(q_st[r0:r0 + (HW - 1) * n + 1:n, :, :], q_src[i, h]).then_inc(q_stacked, 16)

            sp.wait_ge(dve_step, V_MROW)
            sp.dma_start(k_scr[:, MASK_ROW, :].rearrange("h (t k) -> t h k", k=KT),
                         mrow_bf[:, :].unsqueeze(1).to_broadcast([NT, H, KT])).then_inc(mrow_stored, 16)

            sp.wait_ge(ctl_ready, 1)
            first = sp.value_load(ctl[0:1, 0:1], min_val=0, max_val=NB - 1)
            nblk = sp.value_load(ctl[0:1, 2:3], min_val=1, max_val=NB)
            with sp.Fori(0, nblk) as it:
                blk = block_of(it, first)
                sp.wait_ge(v_evac, it + 2)
                sp.dma_start(v_scr[bass.ds(blk * 2, 2), :, :].rearrange("t k n -> k t n"),
                             v_blk[:, :, :, :].rearrange("p t h w -> p t (h w)")).then_inc(v_stored, 16)
                sp.wait_ge(k_split, it * 3 + (3 + 3))
                cols = bass.ds(blk * BLK, BLK)
                for j in range(PARTS):
                    n = PARTS - j
                    sp.dma_start(k_scr[:, K_ROW[j]:K_ROW[j] + HW * n, cols].rearrange("h (w i) k -> h w i k", w=HW),
                                 k_parts[:, j, cols].unsqueeze(1).to_broadcast([P, n, BLK])).then_inc(k_stored, 16)

            v_flat = v_scr.rearrange("t k n -> (t k n)")
            k_src = k_scr.rearrange("(p h) r k -> h r p k", h=2)
            for L in range(STAGES):
                pairs, _, _ = pair_slice(L)
                pairs_n = len(range(NP)[pairs])
                s = max(L - 2, 0)
                with sp.Fori(0, nblk) as it:
                    blk = block_of(it, first)
                    g = sp.snap(it + nblk * L)
                    slot = sp.snap(g & 1)
                    started = sp.snap((g >> 1) * 8 + slot * 4 + 1)
                    t2 = sp.snap((it + nblk * s) * 2)
                    sp.wait_ge(sm_ready, started)
                    for h in range(2):
                        sp.dma_start(k_ring[h * HALF:h * HALF + MAX_ROW, bass.ds(slot, 1), :, h, :]
                                     .rearrange("r a u k -> r (a u) k")[:, 0:pairs_n, :],
                                     k_src[h, :, pairs, bass.ds(blk * BLK, BLK)]).then_inc(k_in, 16)
                    if L >= 2:
                        n0 = s * 2 * (HW + 1)
                        for b in range(2):
                            sp.wait_ge(tile_done, t2 + (b + 1))
                            sp.dma_start(v_ring[:, b, :],
                                         v_scr[bass.ds(blk * 2 + b, 1), :, n0:n0 + 2 * (HW + 1)]
                                         .rearrange("t k n -> k (t n)")).then_inc(v_in[b], 16)

            def load_expert(e, b):
                sp.dma_start(w_gu[:, b, :], gu[bass.ds(e, 1), :, :].rearrange("e d i -> d (e i)")) \
                    .then_inc(w_in[b], 16)
                sp.dma_start(w_dn[:, b, 0:2, :],
                             dn[bass.ds(e, 1), 0:2 * P, :].rearrange("e (c i) o -> i (e c) o", i=P)) \
                    .then_inc(w_in[b], 16)
                sp.dma_start(w_dn[0:ICH[2][1], b, 2, :],
                             dn[bass.ds(e, 1), 2 * P:I, :].rearrange("e i o -> i (e o)")).then_inc(w_in[b], 16)

            load_expert(0, 0)
            load_expert(1, 1)
            with sp.Fori(0, E // 2 - 1) as i:
                for b in range(2):
                    sp.wait_ge(y_ready, i * 4 + (2 * b + 2 + 2))
                    load_expert(i * 2 + (2 + b), b)
            out_v = out.rearrange("a (t p) d -> p (a t) d", p=P)
            for c in range(QC):
                sp.wait_ge(y_used, 2 * (E - 1) + c + 1 + 2)
                sp.dma_start(out_v[:, 4 * c:4 * c + 4, :], acc[:, 4 * c:4 * c + 4, :]).then_inc(out_done, 16)
            sp.wait_ge(out_done, 16 * QC)

        @block.gpsimd
        def _(pool):
            made = 0

            def const(ins):
                nonlocal made
                made += 1
                ins.then_inc(consts, 1)

            const(nc.gpsimd.memset(ident[:, :], 0.0))
            const(nc.gpsimd.memset(neg_ident[:, :], 0.0))
            pool.wait_ge(consts, 2)
            const(nc.gpsimd.affine_select(out=ident[:, :], in_=ident[:, :], compare_op=ALU.not_equal, fill=1.0,
                                          base=0, pattern=[[-1, P]], channel_multiplier=1))
            const(nc.gpsimd.affine_select(out=neg_ident[:, :], in_=neg_ident[:, :], compare_op=ALU.not_equal,
                                          fill=-BIG, base=0, pattern=[[-1, P]], channel_multiplier=1))
            const(nc.gpsimd.memset(ones_f[:, :], 1.0))
            const(nc.gpsimd.memset(ones_b[:, :], 1.0))
            const(nc.gpsimd.memset(zeros_b[:, :], 0.0))
            const(nc.gpsimd.memset(q_rows[:, :], 0.0))
            const(nc.gpsimd.memset(v_blk[:, :, :, :], 1.0))
            const(nc.gpsimd.iota(blk_idx[:, :], pattern=[[1, NB]], base=-(NB - 1), channel_multiplier=0))
            const(nc.gpsimd.iota(e_rank[:, :], pattern=[[-1, ER]], base=ER, channel_multiplier=0))
            const(nc.gpsimd.memset(k_ring[:, :, :, :, :], 0.0))
            pool.wait_ge(consts, N_CONST - 3)
            const(nc.gpsimd.memset(q_rows[0:1, :], 1.0))
            for h in range(2):
                const(nc.gpsimd.memset(k_ring[h * HALF + 32:(h + 1) * HALF, :, :, h, :], -1.0))
            assert made == N_CONST
            for h in range(2):
                nc.gpsimd.memset(q_st[h * HALF + 32:(h + 1) * HALF, :, :], 0.0).then_inc(q_zeroed, 1)
            pool.wait_ge(consts, N_CONST)
            pool.wait_ge(q_zeroed, 2)
            for h in range(2):
                r0 = h * HALF + MASK_ROW
                pool.dma_start(q_st[r0:r0 + 1 + PARTS, :, :],
                               q_rows[:, :].unsqueeze(1).to_broadcast([1 + PARTS, NP, S])).then_inc(q_rows_in, 16)

            pool.wait_ge(ctl_ready, 1)
            first = pool.value_load(ctl[0:1, 0:1], min_val=0, max_val=NB - 1)
            mixed = pool.value_load(ctl[0:1, 1:2], min_val=0, max_val=1)
            nblk = pool.value_load(ctl[0:1, 2:3], min_val=1, max_val=NB)
            with pool.Fori(0, nblk) as it:
                blk = block_of(it, first)
                pool.wait_ge(ctx_in, 16)
                pool.wait_ge(v_mm, it + 1)
                nc.gpsimd.tensor_copy(ctx_blk[:, :], ctx_all[:, bass.ds(blk * BLK, BLK)]).then_inc(ctx_copied, 1)
            pool.wait_ge(k_stored, nblk * (16 * PARTS))
            pool.wait_ge(v_stored, nblk * 16 + 16)
            pool.wait_ge(mrow_stored, 16)
            pool.sem_inc(sm_ready, 4)
            pool.sem_inc(tile_done, 2)

            for L in range(STAGES):
                with pool.If(mixed > 0):
                    with pool.Fori(0, nblk) as it:
                        blk = block_of(it, first)
                        u4 = pool.snap((it + nblk * L) * 4)
                        for b in range(2):
                            pool.wait_ge(sm_ready, u4 + (2 * b + 2))
                            nc.gpsimd.tensor_copy(m_ring[:, b, :, :],
                                                  mask_sb[:, :, bass.ds(blk * BLK + b * KT, KT)]) \
                                .then_inc(mask_tile, 1)
                if L < NP:
                    pool.wait_ge(max_split, 5 * (L + 1))
                    for b in range(4):
                        pool.dma_start(m_scr[L, :, :, 32 * b:32 * b + 32].rearrange("j c q -> c j q"),
                                       max_p[32 * b:32 * b + 2 * QT, :, :]).then_inc(max_stored, 16)
                    pool.wait_ge(max_stored, 64 * (L + 1))
                    for h in range(2):
                        r0 = h * HALF + MAX_ROW
                        pool.dma_start(q_st[r0:r0 + PARTS, L, :].rearrange("j (t q) -> j t q", t=QT),
                                       m_scr[L, :, h:2 * QT:2, :]) \
                            .then_inc(max_in, 16)

        @block.scalar
        def _(act):
            for dst, src in ((wk_sb[:, :], wkT), (bk_sb[:, :], bk),
                             (wv_sb[:, :], wvT), (wo_sb[:, :], woT), (wr_sb[:, :], wrT),
                             (bv_sb[:, :], bv.to_broadcast([P, D])), (bo_sb[:, :], bo.to_broadcast([P, D])),
                             (rb_sb[:, :], rb.to_broadcast([P, ER]))):
                act.dma_start(dst, src).then_inc(small_in, 16)
            act.sem_inc(exp_done, 4)
            act.sem_inc(v_evac, 1)
            done = 0

            def step(ins):
                nonlocal done
                done += 1
                ins.then_inc(act_step, 1)

            def std_dev(v_at):
                act.wait_ge(dve_step, v_at)
                step(nc.scalar.activation(st8[:, 3, :], st8[:, 2, :], ACT.Sqrt))

            std_dev(V_XN1 - 2)
            for c in range(QC):
                act.wait_ge(pe_step, c + 1)
                step(nc.scalar.activation(xnT[:, c * 512:(c + 1) * 512], PS[:, c, :], ACT.Copy))
            for n, (t0, nt) in enumerate(PIECES):
                act.wait_ge(mask_tree, 6 * (n + 1))
                for a, m in enumerate((mask_and, mask_or)):
                    nc.scalar.activation(flags_bf[:, a, t0 * KT:(t0 + nt) * KT],
                                         m[:, t0 * KT // 4:(t0 + nt) * KT // 4].bitcast(U8),
                                         ACT.Copy).then_inc(mask_cast, 1)

            act.wait_ge(ctl_ready, 1)
            first = act.value_load(ctl[0:1, 0:1], min_val=0, max_val=NB - 1)
            nblk = act.value_load(ctl[0:1, 2:3], min_val=1, max_val=NB)
            act.wait_ge(consts, N_CONST)
            act.wait_ge(q_stored, 16)
            with act.Fori(0, nblk) as it:
                blk = block_of(it, first)
                act.wait_ge(k_mm, it + 1)
                nc.scalar.activation(k_parts[:, 0, bass.ds(blk * BLK, BLK)], PS[:, 0, 0:BLK], ACT.Identity,
                                     bias=bk_sb[:, :]).then_inc(k_part0, 1)
                act.wait_ge(v_mm, it + 2)
                act.wait_ge(v_stored, it * 16 + 16)
                nc.scalar.activation(v_blk[:, :, :, 0:HW],
                                     PS[:, 1, 0:2 * D].rearrange("p (t h w) -> p t h w", t=2, w=HW),
                                     ACT.Copy).then_inc(v_evac, 1)

            act.wait_ge(ctx_copied, nblk)
            nc.scalar.activation(ctx_all[:, :], ctx_all[:, :], ACT.Copy, accum_out=csum[:, :]).then_inc(csum_done, 1)
            act.wait_ge(csum_done, 1)

            for L in range(2, STAGES):
                s = L - 2
                with act.Fori(0, nblk) as it:
                    t2 = act.snap((it + nblk * s) * 2)
                    e8 = act.snap(t2 * 4)
                    for b in range(2):
                        act.wait_ge(tile_done, t2 + (b + 1))
                        for v in range(2 * QC):
                            act.wait_ge(sc_ready, e8 + (4 * b + v + 1))
                            nc.scalar.activation(prob[:, b, v, :], PS[:, v % 2, :],
                                                 ACT.Exp).then_inc(exp_done, 1)
                act.wait_ge(tile_done, nblk * (2 * (s + 1)) + 2)
                nc.scalar.activation(o_sb[:, s, :], PS[:, OB + s % 2, :], ACT.Copy).then_inc(o_evac, 1)

            act.wait_ge(pe_step, 17)
            step(nc.scalar.activation(xnT[:, 0:512], PS[:, 0, :], ACT.Copy))
            std_dev(V_XN2 - 2)
            act.wait_ge(pe_step, 20)
            step(nc.scalar.activation(xnT[:, 0:512], PS[:, 0, :], ACT.Copy))
            act.wait_ge(dve_step, V_GAP)
            step(nc.scalar.activation(rs[:, 3, :], rs[:, 2, :], ACT.Exp))
            assert done == 7, done

            with act.Fori(0, E // 2) as i:
                for b in range(2):
                    for c in range(QC):
                        for ic, (_, n) in enumerate(ICH):
                            k = 6 * b + 3 * c + ic
                            act.wait_ge(gu_ready, i * 12 + (k + 1))
                            nc.scalar.activation(sg[0:n, k % 2, :], PS[0:n, k % 2, :], ACT.Silu) \
                                .then_inc(silu_done, 1)

        @block.tensor
        def _(pe):
            done = 0

            def step(ins):
                nonlocal done
                done += 1
                ins.then_inc(pe_step, 1)

            def transpose_tiles(src, c, bank):
                for j in range(4):
                    last = nc.tensor.transpose(PS[:, bank, j * P:(j + 1) * P], src[:, 4 * c + j, :], ident[:, :])
                step(last)

            pe.sem_inc(y_ready, 2)
            pe.sem_inc(v_mm, 1)
            pe.wait_ge(consts, N_CONST)
            pe.wait_ge(dve_step, V_XN1)
            for c in range(QC):
                transpose_tiles(tmp_b, c, c)
            pe.wait_ge(q_weights, 32)
            for c in range(QC):
                pe.wait_ge(act_step, 2 + c)
                step(nc.tensor.matmul(PS[:, 2 + c, :], wq_sb[:, :], xnT[:, c * 512:(c + 1) * 512],
                                      start=True, stop=True))

            for n, (t0, nt) in enumerate(PIECES):
                pe.wait_ge(mask_cast, 2 * (n + 1))
                for a in range(2):
                    for t in range(t0, t0 + nt):
                        last = nc.tensor.matmul(PS[:, 4, t + a * NT:t + a * NT + 1],
                                                flags_bf[:, a, t * KT:(t + 1) * KT], ones_b[:, :],
                                                start=True, stop=True)
            step(last)
            pe.wait_ge(dve_step, V_FLAG)
            step(nc.tensor.transpose(PS[0:NT, 6, 0:P], flag[:, 0, :], ident[:, :]))
            step(nc.tensor.matmul(PS[0:1, 5, 0:2 * NT], ones_f[:, :], flag[:, 1:3, :].rearrange("p a t -> p (a t)"),
                                  start=True, stop=True))

            pe.wait_ge(small_in, 16 * N_SMALL)
            pe.wait_ge(ctl_ready, 1)
            mixed = pe.value_load(ctl[0:1, 1:2], min_val=0, max_val=1)
            nblk = pe.value_load(ctl[0:1, 2:3], min_val=1, max_val=NB)
            with pe.Fori(0, nblk) as it:
                pe.wait_ge(ctx_copied, it + 1)
                pe.wait_ge(k_split, it * 3 + 1)
                nc.tensor.matmul(PS[:, 0, 0:BLK], wk_sb[:, :], ctx_blk[:, :], start=True, stop=True) \
                    .then_inc(k_mm, 1)
                pe.wait_ge(v_evac, it + 1)
                for t in range(2):
                    last = nc.tensor.matmul(PS[:, 1, t * D:(t + 1) * D], ctx_blk[:, t * KT:(t + 1) * KT],
                                            wv_sb[:, :], start=True, stop=True)
                last.then_inc(v_mm, 1)

            pe.wait_ge(k_split, nblk * 3 + 3)
            pe.wait_ge(v_evac, nblk + 1)
            pe.wait_ge(q_stacked, 16 * 2 * 6)
            pe.wait_ge(q_rows_in, 32)

            def attention_blocks(L, masked):
                _, exp_at, max_at = pair_slice(L)
                s = L - 2

                def chunk_scores(k_at, e8, b, c):
                    for h in range(2):
                        pe.wait_ge(exp_done, e8 + (4 * b + 2 * c + h + 1 + 2))
                        last = nc.tensor.matmul(PS[:, h, :], k_tile(k_at, b, exp_at)[:, h, :],
                                                q_st[:, s, c * 512:(c + 1) * 512],
                                                start=True, stop=not masked)
                        if masked:
                            for j in range(4):
                                last = nc.tensor.matmul(PS[:, h, j * P:(j + 1) * P],
                                                        m_ring[:, b, 4 * c + j, :], neg_ident[:, :],
                                                        start=False, stop=j == 3)
                        last.then_inc(sc_ready, 1)

                def max_scores(k_at, u4, b, tiles):
                    for t in tiles:
                        u, j = divmod(t, 4)
                        if j == 0:
                            pe.wait_ge(max_done, u4 + (2 * b + u + 1))
                        scores = PS[:, SM + 2 * u + j // 2, j % 2 * BLK:(j % 2 + 1) * BLK]
                        last = nc.tensor.matmul(scores.rearrange("p (h k) -> p h k", h=2),
                                                q_st[:, L, t * P:(t + 1) * P], k_tile(k_at, b, max_at),
                                                start=True, stop=not masked)
                        if masked:
                            for h in range(2):
                                last = nc.tensor.matmul(scores[:, h * KT:(h + 1) * KT],
                                                        neg_ident[:, :], m_ring[:, b, t, :],
                                                        start=False, stop=h == 1)
                        if j == 3:
                            last.then_inc(sm_ready, 1)

                def attention_block(it, first_of_stage):
                    g = pe.snap(it + nblk * L)
                    u4 = pe.snap(g * 4)
                    k_at = pe.snap((g & 1) * 2)
                    e8 = pe.snap((it + nblk * s) * 8) if L >= 2 else None
                    for b in range(2):
                        if b == 0:
                            pe.wait_ge(k_in, g * 32 + 32)
                        if masked:
                            pe.wait_ge(mask_tile, g * 2 + (b + 1))
                        if exp_at is not None:
                            chunk_scores(k_at, e8, b, 0)
                            if b == 1:
                                weighted_values(s, e8 + (4 + 4), e8 * 2 + 16, 0)
                            elif not first_of_stage:
                                weighted_values(s, e8 + 4, e8 * 2, 1)
                            elif s >= 1:
                                weighted_values(s - 1, e8 + 4, e8 * 2, 1)
                        if max_at is not None:
                            max_scores(k_at, u4, b, range(0, 2))
                        elif b == 0:
                            pe.wait_ge(sc_ready, e8 + 2)
                            pe.sem_inc(sm_ready, 1)
                        else:
                            pe.wait_ge(sc_ready, e8 + 4)
                            pe.sem_inc(sm_ready, 1)
                        if exp_at is not None:
                            chunk_scores(k_at, e8, b, 1)
                        if max_at is not None:
                            max_scores(k_at, u4, b, range(2, QT))
                        elif b == 1:
                            pe.wait_ge(sc_ready, e8 + 8)
                            pe.sem_inc(sm_ready, 2)

                attention_block(0, True)
                with pe.Fori(1, nblk) as it:
                    attention_block(it, False)

            def k_tile(k_at, b, use):
                return k_ring[:, :, :, :, b * KT:(b + 1) * KT].rearrange("p a u h k -> p (a u) h k") \
                    [:, bass.ds(k_at + use, 1), :, :].rearrange("p n h k -> p (n h) k")

            def weighted_values(s, exps, loads, b):
                pe.wait_ge(exp_done, exps)
                pe.wait_ge(v_in[b], loads)
                for g in range(4):
                    h, c = divmod(g, 2)
                    last = nc.tensor.matmul(PS[32 * g:32 * g + HW + 1, OB + s % 2, :],
                                            v_ring[:, b, h * (HW + 1):(h + 1) * (HW + 1)],
                                            prob[:, b, 2 * c + h, :],
                                            start=False, stop=True, skip_group_check=True)
                last.then_inc(tile_done, 1)

            for L in range(STAGES):
                if L >= 2:
                    s = L - 2
                    pe.wait_ge(max_in, 32 * (s + 1))
                    if s >= 2:
                        pe.wait_ge(o_evac, s - 1)
                    nc.tensor.matmul(PS[:, OB + s % 2, :], zeros_b[:, 0:P], zeros_b[:, :], start=True, stop=True,
                                     skip_group_check=True)
                with pe.If(mixed > 0):
                    attention_blocks(L, True)
                with pe.Else():
                    attention_blocks(L, False)
            weighted_values(NP - 1, nblk * (NP * 8) + 4, nblk * (NP * 16), 1)

            pe.wait_ge(o_evac, NP)
            for s in range(NP):
                transpose_tiles(o_sb[:, s, :].rearrange("p (j q) -> p j q", j=4), 0, s)
            pe.wait_ge(dve_step, V_NORM)
            step(nc.tensor.matmul(PS[:, 0, 0:P], csum_b[:, :], wv_sb[:, :], start=True, stop=True))
            pe.wait_ge(dve_step, V_ATT)
            for c in range(QC):
                transpose_tiles(tmp_a, c, c)
            pe.wait_ge(act_step, 4)
            pe.wait_ge(dve_step, V_ATT_T)
            for t in range(QT):
                last = nc.tensor.matmul(PS[:, 2 + t // 4, (t % 4) * P:(t % 4 + 1) * P], xnT[:, t * P:(t + 1) * P],
                                        wo_sb[:, :], start=True, stop=True)
            step(last)
            pe.wait_ge(dve_step, V_XN2)
            for c in range(QC):
                transpose_tiles(tmp_b, c, c)
            pe.wait_ge(act_step, 6)
            pe.wait_ge(dve_step, V_XN2_T)
            for t in range(QT):
                last = nc.tensor.matmul(PS[:, 6, t * ER:(t + 1) * ER], xnT[:, t * P:(t + 1) * P], wr_sb[:, :],
                                        start=True, stop=True)
            step(last)
            assert done == 22, done

            def gate_up(i, b, c):
                for ic, (o, n) in enumerate(ICH):
                    k = 6 * b + 3 * c + ic
                    pe.wait_ge(hid_done, i * 12 + (k + 1))
                    for a in range(2):
                        last = nc.tensor.matmul(PS[0:n, 2 * a + k % 2, :],
                                                w_gu[:, b, a * I + o:a * I + o + n],
                                                xnT[:, c * 512:(c + 1) * 512], start=True, stop=True)
                    last.then_inc(gu_ready, 1)

            def down(i, b, c):
                pe.wait_ge(hid_done, i * 12 + (6 * b + 3 * c + 3 + 2))
                pe.wait_ge(y_used, i * 4 + (2 * b + c + 1))
                for t in range(4):
                    for ic, (_, n) in enumerate(ICH):
                        last = nc.tensor.matmul(PS[:, 4 + c, t * P:(t + 1) * P],
                                                hid[0:n, c, ic, t * P:(t + 1) * P], w_dn[0:n, b, ic, :],
                                                start=ic == 0, stop=ic == NI - 1)
                last.then_inc(y_ready, 1)

            with pe.Fori(0, E // 2) as i:
                pe.wait_ge(w_in[0], i * 48 + 48)
                gate_up(i, 0, 0)
                gate_up(i, 0, 1)
                down(i, 0, 0)
                pe.wait_ge(w_in[1], i * 48 + 48)
                gate_up(i, 1, 0)
                down(i, 0, 1)
                gate_up(i, 1, 1)
                down(i, 1, 0)
                down(i, 1, 1)

        @block.vector
        def _(dve):
            done = 0

            def step(ins, wait=True):
                nonlocal done
                done += 1
                ins.then_inc(dve_step, 1)
                if wait:
                    dve.wait_ge(dve_step, done)

            def per_tile(v):
                return v.unsqueeze(2).to_broadcast([P, QT, D])

            def mark(value):
                assert done == value, (done, value)

            def layernorm(src, root):
                step(nc.vector.tensor_reduce(st8[:, 0, :], src[:, :, :], AX, ALU.add))
                step(nc.vector.tensor_scalar(st8[:, 1, :], st8[:, 0, :], -1.0 / D, None, ALU.mult))
                step(nc.vector.tensor_tensor(tmp_b[:, :, :], src[:, :, :], per_tile(st8[:, 1, :]), ALU.add))
                step(nc.vector.tensor_tensor(tmp_a[:, :, :], tmp_b[:, :, :], tmp_b[:, :, :], ALU.mult))
                step(nc.vector.tensor_reduce(st8[:, 0, :], tmp_a[:, :, :], AX, ALU.add))
                step(nc.vector.tensor_scalar(st8[:, 2, :], st8[:, 0, :], 1.0 / D, 1e-5, ALU.mult, ALU.add))
                dve.wait_ge(act_step, root)
                step(nc.vector.reciprocal(st8[:, 4, :], st8[:, 3, :]))
                step(nc.vector.tensor_tensor(tmp_b[:, :, :], tmp_b[:, :, :], per_tile(st8[:, 4, :]), ALU.mult))

            dve.sem_inc(k_split, 3)
            dve.wait_ge(x_in, 16)
            layernorm(x_sb, 1)
            mark(V_XN1)

            def mask_piece(n):
                t0, nt = PIECES[n]
                w0, w = t0 * KT // 4, nt * KT // 4
                pairs = ((mask_and, tree[0], ALU.bitwise_and), (mask_or, tree[1], ALU.bitwise_or))
                dve.wait_ge(mask_in[n], 16)
                words = mask_sb[:, :, t0 * KT:(t0 + nt) * KT].bitcast(I32)
                for m, (four, _), op in pairs:
                    four = four.rearrange("p (t w) -> p t w", t=4)[:, :, 0:w]
                    nc.vector.tensor_tensor(four, words[:, 0:4, :], words[:, 4:8, :], op).then_inc(mask_tree, 1)
                for a, (m, (four, two), op) in enumerate(pairs):
                    dve.wait_ge(mask_tree, 6 * n + 1 + a)
                    four = four.rearrange("p (t w) -> p t w", t=4)[:, :, 0:w]
                    two = two.rearrange("p (t w) -> p t w", t=2)[:, :, 0:w]
                    nc.vector.tensor_tensor(two, four[:, 0:2, :], four[:, 2:4, :], op).then_inc(mask_tree, 1)
                for a, (m, (_, two), op) in enumerate(pairs):
                    dve.wait_ge(mask_tree, 6 * n + 3 + a)
                    two = two.rearrange("p (t w) -> p t w", t=2)[:, :, 0:w]
                    nc.vector.tensor_tensor(m[:, w0:w0 + w], two[:, 0, :], two[:, 1, :], op).then_inc(mask_tree, 1)

            mask_piece(0)
            mask_piece(1)

            dve.wait_ge(q_weights, 32)
            dve.wait_ge(pe_step, 4)
            q32 = tmp_b[:, :, :].rearrange("p t d -> p (t d)")
            rest = tmp_a[:, :, :].rearrange("p t d -> p (t d)")
            step(nc.vector.tensor_scalar(q32, PS[:, 2:4, :].rearrange("p c q -> p (c q)"), bq_sb[:, :], None, ALU.add))
            step(nc.vector.tensor_copy(q_parts[:, 0, :], q32))
            step(nc.vector.tensor_tensor(rest, q32, q_parts[:, 0, :], ALU.subtract))
            step(nc.vector.tensor_copy(q_parts[:, 1, :], rest))
            step(nc.vector.tensor_tensor(q_parts[:, 2, :], rest, q_parts[:, 1, :], ALU.subtract))
            mark(V_QPARTS)

            for n in range(2, len(PIECES)):
                mask_piece(n)

            dve.wait_ge(pe_step, 5)
            step(nc.vector.tensor_scalar(flag[:, 0, :], PS[:, 4, 0:NT], P - 0.5, None, ALU.is_ge))
            step(nc.vector.tensor_scalar(flag[:, 1, :], flag[:, 0, :], -1.0, 1.0, ALU.mult, ALU.add))
            step(nc.vector.scalar_tensor_tensor(flag[:, 2, :], PS[:, 4, NT:2 * NT], 0.5, flag[:, 0, :],
                                                ALU.is_ge, ALU.subtract))
            mark(V_FLAG)
            dve.wait_ge(pe_step, 7)
            step(nc.vector.tensor_scalar(mrow_bf[:, :], PS[0:NT, 6, 0:KT], -BIG, None, ALU.mult))
            mark(V_MROW)
            dve.wait_ge(consts, N_CONST)
            step(nc.vector.tensor_reduce(row[:, 0, :], PS[0:1, 5, 0:2 * NT].rearrange("p (n t) -> p n t", t=2),
                                         AX, ALU.max))
            step(nc.vector.tensor_copy(blk_idx_f[:, :], blk_idx[:, :]))
            step(nc.vector.scalar_tensor_tensor(row[:, 1, 0:NB], row[:, 0, 0:NB], 0.5, blk_idx_f[:, :],
                                                ALU.is_ge, ALU.mult))
            step(nc.vector.tensor_reduce(row[:, 2, 0:1], row[:, 1, 0:NB], AX, ALU.min))
            step(nc.vector.tensor_scalar(ctl[:, 0:1], row[:, 2, 0:1], float(NB - 1), None, ALU.add))
            step(nc.vector.tensor_reduce(row[:, 3, 0:1], row[:, 0, NB:2 * NB], AX, ALU.max))
            step(nc.vector.tensor_scalar(ctl[:, 2:3], row[:, 2, 0:1], -1.0, 1.0, ALU.mult, ALU.add))
            nc.vector.tensor_scalar(ctl[:, 1:2], row[:, 3, 0:1], 0.5, None, ALU.is_ge).then_inc(ctl_ready, 1)

            dve.wait_ge(mask_cast, 2 * len(PIECES))
            dve.wait_ge(small_in, 16 * N_SMALL)
            step(nc.vector.tensor_tensor(acc[:, :, :], x_sb[:, :, :],
                                         bo_sb[:, :].unsqueeze(1).to_broadcast([P, QT, D]), ALU.add))
            step(nc.vector.tensor_copy(e_rank_f[:, :], e_rank[:, :]))
            dve.wait_ge(small_in, 16 * N_SMALL)
            dve.wait_ge(ctl_ready, 1)
            dve.wait_ge(q_stored, 16)
            first = dve.value_load(ctl[0:1, 0:1], min_val=0, max_val=NB - 1)
            nblk = dve.value_load(ctl[0:1, 2:3], min_val=1, max_val=NB)
            with dve.Fori(0, nblk) as it:
                blk = block_of(it, first)
                it3 = dve.snap(it * 3 + 3)
                cols = bass.ds(blk * BLK, BLK)
                dve.wait_ge(k_part0, it + 1)
                dve.wait_ge(k_split, it3)
                nc.vector.scalar_tensor_tensor(kr1[:, :], PS[:, 0, 0:BLK], bk_sb[:, :], k_parts[:, 0, cols],
                                               ALU.add, ALU.subtract).then_inc(k_split, 1)
                dve.wait_ge(k_split, it3 + 1)
                nc.vector.tensor_copy(k_parts[:, 1, cols], kr1[:, :]).then_inc(k_split, 1)
                dve.wait_ge(k_split, it3 + 2)
                nc.vector.tensor_tensor(k_parts[:, 2, cols], kr1[:, :], k_parts[:, 1, cols], ALU.subtract) \
                    .then_inc(k_split, 1)

            nc.vector.memset(maxT[:, :], 0.0).then_inc(max_init, 1)
            nc.vector.memset(run_max[:, :], FLOOR).then_inc(max_init, 1)
            dve.sem_inc(max_done, 2)
            dve.sem_inc(max_fold, 2)
            for L in range(NP):
                if L:
                    nc.vector.memset(run_max[:, 0:2 * QT], FLOOR).then_inc(max_init, 1)
                dve.wait_ge(max_init, 2 + L)
                with dve.Fori(0, nblk) as it:
                    g = dve.snap(it + nblk * L)
                    u4 = dve.snap(g * 4)
                    dve.wait_ge(max_fold, g * 2 + 2)
                    for b in range(2):
                        for u in range(2):
                            dve.wait_ge(sm_ready, u4 + (2 * b + u + 1 + 4))
                            nc.vector.tensor_reduce(tile_max[:, b, QT * u:QT * (u + 1)],
                                                    PS[:, SM + 2 * u:SM + 2 * u + 2, :]
                                                    .rearrange("p n (m k) -> p (n m) k", k=KT),
                                                    AX, ALU.max).then_inc(max_done, 1)
                    dve.wait_ge(max_done, u4 + 4 + 2)
                    nc.vector.tensor_tensor(tile_max[:, 0, :], tile_max[:, 0, :], tile_max[:, 1, :], ALU.max) \
                        .then_inc(max_fold, 1)
                    dve.wait_ge(max_fold, g * 2 + (1 + 2))
                    nc.vector.tensor_tensor(run_max[:, 0:2 * QT], run_max[:, 0:2 * QT], tile_max[:, 0, :], ALU.max) \
                        .then_inc(max_fold, 1)
                dve.wait_ge(max_fold, nblk * (2 * (L + 1)) + 2)
                nc.vector.transpose(maxT[:, :], run_max[:, :]).then_inc(max_split, 1)
                dve.wait_ge(max_split, 5 * L + 1)
                if L:
                    dve.wait_ge(max_stored, 64 * L)
                nc.vector.tensor_copy(max_p[:, 0, :], maxT[:, :]).then_inc(max_split, 1)
                dve.wait_ge(max_split, 5 * L + 2)
                nc.vector.tensor_tensor(max_r[:, :], maxT[:, :], max_p[:, 0, :], ALU.subtract).then_inc(max_split, 1)
                dve.wait_ge(max_split, 5 * L + 3)
                nc.vector.tensor_copy(max_p[:, 1, :], max_r[:, :]).then_inc(max_split, 1)
                dve.wait_ge(max_split, 5 * L + 4)
                nc.vector.tensor_tensor(max_p[:, 2, :], max_r[:, :], max_p[:, 1, :], ALU.subtract) \
                    .then_inc(max_split, 1)

            dve.wait_ge(csum_done, 1)
            step(nc.vector.tensor_copy(csum_b[:, :], csum[:, :].to_broadcast([P, P])))
            dve.wait_ge(pe_step, 15)
            o_t = PS[:, :, :].rearrange("p s (n r) -> p (s n) r", r=32)
            step(nc.vector.tensor_scalar(none_l[:, :], o_t[:, :, HW], 0.0, None, ALU.is_equal))
            step(nc.vector.tensor_tensor(den[:, :], o_t[:, :, HW], none_l[:, :], ALU.add))
            step(nc.vector.reciprocal(den[:, :], den[:, :]))

            def heads_of(v, h, c):
                return v[:, 4 * c:4 * c + 4, :].rearrange("p j (s h w) -> p s j h w", h=2, w=HW)[:, :, :, h, :]

            def of_group(v, h, c):
                return v[:, :].rearrange("p (s j g) -> p s j g", s=NP, g=4)[:, :, :, 2 * h + c] \
                    .unsqueeze(3).to_broadcast([P, NP, 4, HW])

            for h in range(2):
                for c in range(QC):
                    step(nc.vector.tensor_tensor(
                        heads_of(tmp_a, h, c),
                        PS[:, :, :].rearrange("p s (j g r) -> p s j g r", j=4, r=32)[:, :, :, 2 * h + c, 0:HW],
                        of_group(den, h, c), ALU.mult))
            mark(V_NORM)
            dve.wait_ge(pe_step, 16)
            step(nc.vector.tensor_scalar(csum_b[:, :], PS[:, 0, 0:D], 1.0 / T, None, ALU.mult))
            for h in range(2):
                for c in range(QC):
                    step(nc.vector.tensor_tensor(
                        heads_of(tmp_b, h, c), of_group(none_l, h, c),
                        csum_b[:, :].rearrange("p (s h w) -> p s h w", h=2, w=HW)[:, :, h, :]
                        .unsqueeze(2).to_broadcast([P, NP, 4, HW]), ALU.mult))
            step(nc.vector.tensor_tensor(tmp_a[:, :, :], tmp_a[:, :, :], tmp_b[:, :, :], ALU.add))
            step(nc.vector.tensor_tensor(tmp_a[:, :, :], tmp_a[:, :, :],
                                         bv_sb[:, :].unsqueeze(1).to_broadcast([P, QT, D]), ALU.add))
            mark(V_ATT)
            dve.wait_ge(pe_step, 18)
            step(nc.vector.tensor_copy(xnT[:, 512:1024], PS[:, 1, :]))
            mark(V_ATT_T)
            dve.wait_ge(pe_step, 19)
            flat = acc[:, :, :].rearrange("p t d -> p (t d)")
            step(nc.vector.scalar_tensor_tensor(flat, PS[:, 2:4, :].rearrange("p c q -> p (c q)"),
                                                float(HW) ** -0.5, flat, ALU.mult, ALU.add))
            layernorm(acc, 5)
            mark(V_XN2)
            dve.wait_ge(pe_step, 21)
            step(nc.vector.tensor_copy(xnT[:, 512:1024], PS[:, 1, :]))
            mark(V_XN2_T)

            def per_expert(v):
                return v.unsqueeze(2).to_broadcast([P, QT, ER])

            rank = e_rank_f[:, :].unsqueeze(1).to_broadcast([P, QT, ER])

            def pick(logits, top, hot, tmp):
                step(nc.vector.tensor_reduce(top, logits, AX, ALU.max))
                step(nc.vector.tensor_tensor(hot, logits, per_expert(top), ALU.is_equal))
                step(nc.vector.tensor_tensor(tmp, hot, rank, ALU.mult))
                step(nc.vector.tensor_reduce(rs[:, 1, :], tmp, AX, ALU.max))
                step(nc.vector.tensor_tensor(hot, tmp, per_expert(rs[:, 1, :]), ALU.is_equal))

            dve.wait_ge(pe_step, 22)
            step(nc.vector.tensor_tensor(rt[:, 0, :, :], PS[:, 6, 0:QT * ER].rearrange("p (t e) -> p t e", e=ER),
                                         rb_sb[:, :].unsqueeze(1).to_broadcast([P, QT, ER]), ALU.add))
            pick(rt[:, 0, :, :], rs[:, 0, :], rt[:, 1, :, :], rt[:, 2, :, :])
            step(nc.vector.scalar_tensor_tensor(rt[:, 2, :, :], rt[:, 1, :, :], -BIG, rt[:, 0, :, :],
                                                ALU.mult, ALU.add))
            pick(rt[:, 2, :, :], rs[:, 4, :], rt[:, 3, :, :], rt[:, 4, :, :])
            step(nc.vector.tensor_tensor(rs[:, 2, :], rs[:, 4, :], rs[:, 0, :], ALU.subtract))
            mark(V_GAP)
            dve.wait_ge(act_step, 7)
            step(nc.vector.tensor_scalar(rs[:, 1, :], rs[:, 3, :], 1.0, None, ALU.add))
            step(nc.vector.reciprocal(rs[:, 1, :], rs[:, 1, :]))
            step(nc.vector.tensor_tensor(rs[:, 5, :], rs[:, 3, :], rs[:, 1, :], ALU.mult))
            step(nc.vector.tensor_tensor(rt[:, 1, :, :], rt[:, 1, :, :], per_expert(rs[:, 1, :]), ALU.mult))
            step(nc.vector.tensor_tensor(rt[:, 3, :, :], rt[:, 3, :, :], per_expert(rs[:, 5, :]), ALU.mult))
            step(nc.vector.tensor_tensor(w_all[:, 1:E, :], rt[:, 1, :, :].rearrange("p t e -> p e t"),
                                         rt[:, 3, :, :].rearrange("p t e -> p e t"), ALU.add))
            step(nc.vector.memset(w_all[:, 0, :], 1.0))

            dve.sem_inc(hid_done, 2)
            dve.sem_inc(y_used, 2)
            with dve.Fori(0, E // 2) as i:
                dve.wait_ge(y_used, i * 4 + 2)
                nc.vector.tensor_copy(w_cur[:, :, :], w_all[:, bass.ds(i * 2, 2), :]).then_inc(w_copied, 1)

                def hidden(b, c):
                    dve.wait_ge(y_ready, i * 4 + (2 * b + c + 1))
                    for ic, (_, n) in enumerate(ICH):
                        k = 6 * b + 3 * c + ic
                        dve.wait_ge(silu_done, i * 12 + (k + 1))
                        nc.vector.tensor_tensor(hid[0:n, c, ic, :], sg[0:n, k % 2, :], PS[0:n, 2 + k % 2, :],
                                                ALU.mult).then_inc(hid_done, 1)

                def add_output(b, c):
                    dve.wait_ge(y_ready, i * 4 + (2 * b + c + 1 + 2))
                    dve.wait_ge(y_used, i * 4 + (2 * b + c + 1))
                    for t in range(4):
                        tile = acc[:, 4 * c + t, :]
                        last = nc.vector.scalar_tensor_tensor(tile, PS[:, 4 + c, t * P:(t + 1) * P],
                                                              w_cur[:, b, 4 * c + t:4 * c + t + 1], tile,
                                                              ALU.mult, ALU.add)
                    last.then_inc(y_used, 1)

                hidden(0, 0)
                hidden(0, 1)
                dve.wait_ge(w_copied, i + 1)
                add_output(0, 0)
                hidden(1, 0)
                add_output(0, 1)
                hidden(1, 1)
                add_output(1, 0)
                add_output(1, 1)


def kernel(**inputs):
    import numpy as np
    import concourse.bacc as bacc
    from concourse.bass_utils import run_bass_kernel_spmd as run

    a = {n: np.asarray(v) for n, v in inputs.items()}
    at, ff = "L0_xattn_", "L0_ffn_"
    x = a["x"][0]
    S, D = x.shape
    T = a["ctx_1024"].shape[1]
    front = padded_keys(T) - T
    I = a[ff + "sg"].shape[0]
    g = np.concatenate([a[ff + "sg"][None], a[ff + "rg"]]).transpose(0, 2, 1)
    u = np.concatenate([a[ff + "su"][None], a[ff + "ru"]]).transpose(0, 2, 1)
    arrays = {
        "x": x,
        "ctxT": np.pad(a["ctx_1024"][0].T, ((0, 0), (front, 0))),
        "mask": np.pad(a["mask_SxS2_bk1"], ((0, 0), (front, 0)), constant_values=True),
        "wqT": a[at + "Wq"].reshape(D, D).T, "bq": a[at + "bq"].reshape(D, 1),
        "wkT": a[at + "Wk"].reshape(D, D).T, "bk": a[at + "bk"].reshape(D, 1),
        "wvT": a[at + "Wv"].reshape(D, D).T, "bv": a[at + "bv"].reshape(1, D),
        "woT": a[at + "Wo"].reshape(D, D).T, "bo": a[at + "bo"].reshape(1, D),
        "gu": np.concatenate([g, u], axis=2),
        "dn": np.concatenate([a[ff + "sd"][None], a[ff + "rd"]]).transpose(0, 2, 1),
        "wrT": a[ff + "wr"].T, "rb": a[ff + "rb"].reshape(1, -1),
    }
    arrays = {n: np.ascontiguousarray(v) for n, v in arrays.items()}
    nc = bacc.Bacc("TRN2", target_bir_lowering=False, num_devices=1)
    args = {n: nc.dram_tensor(f"in_{n}", v.shape, mybir.dt.from_np(v.dtype), kind="ExternalInput").ap()
            for n, v in arrays.items()}
    out = nc.dram_tensor("out", (1, S, D), F32, kind="ExternalOutput").ap()
    xattn_moe(nc, *args.values(), out, T)
    r = run(nc, [{f"in_{n}": v for n, v in arrays.items()}], core_ids=[0])
    return r.results[0]["out"]
```

```python
from contextlib import ExitStack

import concourse.bass as bass
from concourse import mybir

F32 = mybir.dt.float32
BF16 = mybir.dt.bfloat16
I32 = mybir.dt.int32
U8 = mybir.dt.uint8
F8 = mybir.dt.float8e4
F32R = mybir.dt.float32r
ALU = mybir.AluOpType
ACT = mybir.ActivationFunctionType
AX = mybir.AxisListType.X

P = 128
KT = 128
BLK = 2 * KT
HW = 8
PARTS = 3
K_ROW = (0, 3 * HW, 5 * HW)
MASK_ROW = 6 * HW
MAX_ROW = MASK_ROW + 1
HALF = 64
BIG = float(2.0 ** 100)
BYTE_ONE = 2.0 ** -9
HIGH_BITS = -4096
FLOOR = -1.0e9


def padded_keys(T):
    return -(-T // BLK) * BLK


def xattn_moe(nc, x, ctxT, mask, wqT, bq, wkT, bk, wvT, bv, woT, bo, gu, dn, wrT, rb, out, T):
    S, D = x.shape
    QT = S // P
    QC = S // 512
    TP = ctxT.shape[1]
    NB = TP // BLK
    NT = TP // KT
    H = D // HW
    NP = H // 2
    STAGES = NP + 2
    E, _, I2 = gu.shape
    I = I2 // 2
    ER = E - 1
    ICH = [(o, min(P, I - o)) for o in range(0, I, P)]
    NI = len(ICH)
    PIECES = [(t, min(8, NT - t)) for t in range(0, NT, 8)]
    assert D == P and QC == 2 and QT == 8 and H == 16 and NI == 3 and E % 2 == 0 and NB % 2 == 0

    k_scr = nc.dram_tensor("k_scr", (H, MAX_ROW, TP), BF16, kind="Internal").ap()
    v_scr = nc.dram_tensor("v_scr", (NT, KT, H * (HW + 1)), F32, kind="Internal").ap()
    q_scr = nc.dram_tensor("q_scr", (H, MASK_ROW, S), BF16, kind="Internal").ap()
    m_scr = nc.dram_tensor("m_scr", (NP, PARTS, 2 * QT, P), BF16, kind="Internal").ap()

    with ExitStack() as ctx:
        def sb(name, shape, dt=F32):
            return ctx.enter_context(nc.sbuf_tensor(name, shape, dt))

        def sem(name):
            return ctx.enter_context(nc.semaphore(name))

        PS = ctx.enter_context(nc.psum_tensor("PS", [P, 8, 512], F32))
        SM = 2
        OB = 6

        x_sb = sb("x_sb", [P, QT, D])
        mask_sb = sb("mask_sb", [P, QT, TP], U8)
        mask_f8 = mask_sb[:, :, :].bitcast(F8)
        o_sb = sb("o_sb", [P, NP, 512])
        m_ring = sb("m_ring", [P, 2, QT, KT], BF16)
        acc = x_sb
        ctx_all = sb("ctx_all", [P, TP])
        prob = ctx_all[:, 0:4096].rearrange("p (b v q) -> p b v q", b=2, v=2 * QC)
        k_parts = sb("k_parts", [P, PARTS, TP], BF16)
        late = k_parts[:, :, :].rearrange("p j k -> p (j k)").bitcast(F32)
        sizes = (2 * NI * 512, 3 * 512, 2 * I2, 2 * NI * D, 6 * QT * ER, NP * 16, NP * 16)
        ends = [sum(sizes[:n + 1]) for n in range(len(sizes))]
        hid = late[:, 0:ends[0]].rearrange("p (c n q) -> p c n q", c=2, n=NI)
        sg = late[:, ends[0]:ends[1]].rearrange("p (b q) -> p b q", b=3)
        w_gu = late[:, ends[1]:ends[2]].rearrange("p (b i) -> p b i", b=2)
        w_dn = late[:, ends[2]:ends[3]].rearrange("p (b n o) -> p b n o", b=2, n=NI)
        rt = late[:, ends[3]:ends[4]].rearrange("p (n t e) -> p n t e", n=6, t=QT)
        none_l = late[:, ends[4]:ends[5]]
        den = late[:, ends[5]:ends[6]]
        xn_parts = sb("xn_parts", [P, 2, S], F32R)
        w_parts = sb("w_parts", [P, 2, 2, I2], F32R)
        o_flat = o_sb[:, :, :].rearrange("p s q -> p (s q)")
        q_parts = o_flat[:, 0:PARTS * S // 2].bitcast(BF16).rearrange("p (j q) -> p j q", j=PARTS)
        w_high = o_flat[:, 0:I2]
        q_st = sb("q_st", [P, NP, S], BF16)
        wq_sb = sb("wq_sb", [P, D])
        wk_sb = sb("wk_sb", [P, D])
        wv_sb = sb("wv_sb", [P, D])
        wo_sb = sb("wo_sb", [P, D])
        wr_sb = sb("wr_sb", [P, ER])
        bq_sb = sb("bq_sb", [P, 1])
        bk_sb = sb("bk_sb", [P, 1])
        bv_sb = sb("bv_sb", [P, D])
        bo_sb = sb("bo_sb", [P, D])
        rb_sb = sb("rb_sb", [P, ER])
        ident = sb("ident", [P, P])
        neg_ident = sb("neg_ident", [P, P], BF16)
        ones_f = sb("ones_f", [P, 1])
        ones_8 = sb("ones_8", [P, 1], F8)
        zeros_b = sb("zeros_b", [P, 512], BF16)
        q_rows = sb("q_rows", [1 + PARTS, S], BF16)
        blk_idx = sb("blk_idx", [1, NB], I32)
        blk_idx_f = sb("blk_idx_f", [1, NB])
        e_rank = sb("e_rank", [P, ER], I32)
        e_rank_f = sb("e_rank_f", [P, ER])
        tmp_a = sb("tmp_a", [P, QT, D])
        tmp_b = sb("tmp_b", [P, QT, D])
        xnT = sb("xnT", [P, S])
        st8 = sb("st8", [P, 6, QT])
        flag = sb("flag", [P, 3, NT])
        row = sb("row", [1, 4, 2 * NB])
        ctl = sb("ctl", [1, 3], I32)
        mrow_bf = sb("mrow_bf", [NT, KT], BF16)
        ctx_blk = sb("ctx_blk", [P, BLK])
        kr1 = sb("kr1", [P, BLK])
        v_blk = sb("v_blk", [P, 2, H, HW + 1])
        csum = sb("csum", [P, 1])
        csum_b = sb("csum_b", [P, P])
        k_ring = sb("k_ring", [P, 2, 2, 2, BLK], BF16)
        v_ring = sb("v_ring", [P, 2, 2 * (HW + 1)])
        tile_max = sb("tile_max", [P, 2, 2 * QT])
        run_max = sb("run_max", [P, 32])
        maxT = sb("maxT", [P, 32])
        max_r = sb("max_r", [P, 32])
        max_p = sb("max_p", [P, PARTS, 32], BF16)
        rs = sb("rs", [P, 6, QT])
        w_all = sb("w_all", [P, E, QT])
        w_cur = sb("w_cur", [P, 2, QT])

        x_in = sem("x_in")
        mask_in = [sem(f"mask_in{n}") for n in range(len(PIECES))]
        ctx_in = sem("ctx_in")
        q_weights = sem("q_weights")
        small_in = sem("small_in")
        consts = sem("consts")
        dve_step = sem("dve_step")
        act_step = sem("act_step")
        pe_step = sem("pe_step")
        csum_done = sem("csum_done")
        q_stored = sem("q_stored")
        q_stacked = sem("q_stacked")
        q_rows_in = sem("q_rows_in")
        mrow_stored = sem("mrow_stored")
        ctl_ready = sem("ctl_ready")
        ctx_copied = sem("ctx_copied")
        k_mm = sem("k_mm")
        v_mm = sem("v_mm")
        k_part0 = sem("k_part0")
        k_split = sem("k_split")
        v_evac = sem("v_evac")
        v_stored = sem("v_stored")
        k_stored = sem("k_stored")
        q_zeroed = sem("q_zeroed")
        k_in = sem("k_in")
        v_in = [sem("v_in0"), sem("v_in1")]
        tile_done = sem("tile_done")
        mask_tile = sem("mask_tile")
        sc_ready = sem("sc_ready")
        exp_done = sem("exp_done")
        sm_ready = sem("sm_ready")
        max_done = sem("max_done")
        max_init = sem("max_init")
        max_fold = sem("max_fold")
        max_split = sem("max_split")
        max_stored = sem("max_stored")
        max_in = sem("max_in")
        o_evac = sem("o_evac")
        w_split = sem("w_split")
        w_in = [sem("w_in0"), sem("w_in1")]
        gu_ready = sem("gu_ready")
        silu_done = sem("silu_done")
        hid_done = sem("hid_done")
        w_copied = sem("w_copied")
        y_ready = sem("y_ready")
        y_used = sem("y_used")
        out_done = sem("out_done")

        N_CONST = 15
        N_SMALL = 8

        def pair_slice(L):
            if L < 2:
                return slice(L, L + 3, 2), None, 0
            if L < NP:
                return slice(L - 2, L + 1, 2), 0, 1
            return slice(L - 4, L - 1, 2), 1, None

        V_XN1 = 8
        V_QPARTS = 13
        V_FLAG = 16
        V_MROW = 17
        V_NORM_A = 34
        V_MEAN = 42
        V_ATT = 61
        V_ATT_T = 62
        V_XN2 = 71
        V_XN2_T = 72
        V_SPLIT = 75
        V_GAP = 88

        def block_of(it, first):
            return nc.s_assert_within(it + first, 0, NB - 1, skip_runtime_bounds_check_because="it < NB - first")

        block = ctx.enter_context(nc.Block())

        @block.sync
        def _(sp):
            sp.sem_inc(v_stored, 16)
            sp.dma_start(x_sb[:, :, :], x.rearrange("(t p) d -> p t d", p=P)).then_inc(x_in, 16)
            sp.dma_start(wq_sb[:, :], wqT).then_inc(q_weights, 16)
            sp.dma_start(bq_sb[:, :], bq).then_inc(q_weights, 16)
            for n, (t0, nt) in enumerate(PIECES):
                cols = slice(t0 * KT, (t0 + nt) * KT)
                sp.dma_start(mask_sb[:, :, cols], mask.rearrange("(t p) k -> p t k", p=P)[:, :, cols]) \
                    .then_inc(mask_in[n], 16)
            sp.dma_start(ctx_all[:, :], ctxT).then_inc(ctx_in, 16)

            sp.wait_ge(dve_step, V_MROW)
            sp.dma_start(k_scr[:, MASK_ROW, :].rearrange("h (t k) -> t h k", k=KT),
                         mrow_bf[:, :].unsqueeze(1).to_broadcast([NT, H, KT])).then_inc(mrow_stored, 16)

            sp.wait_ge(ctl_ready, 1)
            first = sp.value_load(ctl[0:1, 0:1], min_val=0, max_val=NB - 2)
            nblk = sp.value_load(ctl[0:1, 2:3], min_val=2, max_val=NB)
            with sp.Fori(0, nblk) as it:
                blk = block_of(it, first)
                sp.wait_ge(v_evac, it + 2)
                sp.dma_start(v_scr[bass.ds(blk * 2, 2), :, :].rearrange("t k n -> k t n"),
                             v_blk[:, :, :, :].rearrange("p t h w -> p t (h w)")).then_inc(v_stored, 16)
                sp.wait_ge(k_split, it * 3 + (3 + 3))
                cols = bass.ds(blk * BLK, BLK)
                for j in range(PARTS):
                    n = PARTS - j
                    sp.dma_start(k_scr[:, K_ROW[j]:K_ROW[j] + HW * n, cols].rearrange("h (w i) k -> h w i k", w=HW),
                                 k_parts[:, j, cols].unsqueeze(1).to_broadcast([P, n, BLK])).then_inc(k_stored, 16)

            v_flat = v_scr.rearrange("t k n -> (t k n)")
            k_src = k_scr.rearrange("(p h) r k -> h r p k", h=2)
            for L in range(STAGES):
                pairs, _, _ = pair_slice(L)
                pairs_n = len(range(NP)[pairs])
                s = max(L - 2, 0)
                with sp.Fori(0, nblk) as it:
                    blk = block_of(it, first)
                    g = sp.snap(it + nblk * L)
                    slot = sp.snap(g & 1)
                    started = sp.snap((g >> 1) * 8 + slot * 4 + 1)
                    t2 = sp.snap((it + nblk * s) * 2)
                    sp.wait_ge(sm_ready, started)
                    for h in range(2):
                        sp.dma_start(k_ring[h * HALF:h * HALF + MAX_ROW, bass.ds(slot, 1), :, h, :]
                                     .rearrange("r a u k -> r (a u) k")[:, 0:pairs_n, :],
                                     k_src[h, :, pairs, bass.ds(blk * BLK, BLK)]).then_inc(k_in, 16)
                    if L >= 2:
                        n0 = s * 2 * (HW + 1)
                        for b in range(2):
                            sp.wait_ge(tile_done, t2 + (b + 1))
                            sp.dma_start(v_ring[:, b, :],
                                         v_scr[bass.ds(blk * 2 + b, 1), :, n0:n0 + 2 * (HW + 1)]
                                         .rearrange("t k n -> k (t n)")).then_inc(v_in[b], 16)

            def load_expert(e, b):
                sp.dma_start(w_gu[:, b, :], gu[bass.ds(e, 1), :, :].rearrange("e d i -> d (e i)")) \
                    .then_inc(w_in[b], 16)
                sp.dma_start(w_dn[:, b, 0:2, :],
                             dn[bass.ds(e, 1), 0:2 * P, :].rearrange("e (c i) o -> i (e c) o", i=P)) \
                    .then_inc(w_in[b], 16)
                sp.dma_start(w_dn[0:ICH[2][1], b, 2, :],
                             dn[bass.ds(e, 1), 2 * P:I, :].rearrange("e i o -> i (e o)")).then_inc(w_in[b], 16)

            load_expert(0, 0)
            load_expert(1, 1)
            with sp.Fori(0, E // 2 - 1) as i:
                for b in range(2):
                    sp.wait_ge(y_ready, i * 4 + (2 * b + 2 + 2))
                    load_expert(i * 2 + (2 + b), b)
            out_v = out.rearrange("a (t p) d -> p (a t) d", p=P)
            for c in range(QC):
                sp.wait_ge(y_used, 2 * (E - 1) + c + 1 + 2)
                sp.dma_start(out_v[:, 4 * c:4 * c + 4, :], acc[:, 4 * c:4 * c + 4, :]).then_inc(out_done, 16)
            sp.wait_ge(out_done, 16 * QC)

        @block.gpsimd
        def _(pool):
            made = 0

            def const(ins):
                nonlocal made
                made += 1
                ins.then_inc(consts, 1)

            const(nc.gpsimd.memset(ident[:, :], 0.0))
            const(nc.gpsimd.memset(neg_ident[:, :], 0.0))
            pool.wait_ge(consts, 2)
            const(nc.gpsimd.affine_select(out=ident[:, :], in_=ident[:, :], compare_op=ALU.not_equal, fill=1.0,
                                          base=0, pattern=[[-1, P]], channel_multiplier=1))
            const(nc.gpsimd.affine_select(out=neg_ident[:, :], in_=neg_ident[:, :], compare_op=ALU.not_equal,
                                          fill=-BIG, base=0, pattern=[[-1, P]], channel_multiplier=1))
            const(nc.gpsimd.memset(ones_f[:, :], 1.0))
            const(nc.gpsimd.memset(ones_8[:, :], 1.0))
            const(nc.gpsimd.memset(zeros_b[:, :], 0.0))
            const(nc.gpsimd.memset(q_rows[:, :], 0.0))
            const(nc.gpsimd.memset(v_blk[:, :, :, :], 1.0))
            const(nc.gpsimd.iota(blk_idx[:, :], pattern=[[1, NB]], base=-(NB - 2), channel_multiplier=0))
            const(nc.gpsimd.iota(e_rank[:, :], pattern=[[-1, ER]], base=ER, channel_multiplier=0))
            const(nc.gpsimd.memset(k_ring[:, :, :, :, :], 0.0))
            pool.wait_ge(consts, N_CONST - 3)
            const(nc.gpsimd.memset(q_rows[0:1, :], 1.0))
            for h in range(2):
                const(nc.gpsimd.memset(k_ring[h * HALF + 32:(h + 1) * HALF, :, :, h, :], -1.0))
            assert made == N_CONST
            for h in range(2):
                nc.gpsimd.memset(q_st[h * HALF + 32:(h + 1) * HALF, :, :], 0.0).then_inc(q_zeroed, 1)
            pool.wait_ge(consts, N_CONST)
            pool.wait_ge(q_zeroed, 2)
            for h in range(2):
                r0 = h * HALF + MASK_ROW
                pool.dma_start(q_st[r0:r0 + 1 + PARTS, :, :],
                               q_rows[:, :].unsqueeze(1).to_broadcast([1 + PARTS, NP, S])).then_inc(q_rows_in, 16)

            pool.wait_ge(ctl_ready, 1)
            first = pool.value_load(ctl[0:1, 0:1], min_val=0, max_val=NB - 2)
            nblk = pool.value_load(ctl[0:1, 2:3], min_val=2, max_val=NB)
            with pool.Fori(0, nblk) as it:
                blk = block_of(it, first)
                pool.wait_ge(ctx_in, 16)
                pool.wait_ge(v_mm, it + 1)
                nc.gpsimd.tensor_copy(ctx_blk[:, :], ctx_all[:, bass.ds(blk * BLK, BLK)]).then_inc(ctx_copied, 1)
            mixed = pool.value_load(ctl[0:1, 1:2], min_val=0, max_val=1)
            pool.wait_ge(k_stored, nblk * (16 * PARTS))
            pool.wait_ge(v_stored, nblk * 16 + 16)
            pool.wait_ge(mrow_stored, 16)
            pool.sem_inc(sm_ready, 4)
            pool.sem_inc(tile_done, 2)

            for L in range(STAGES):
                with pool.If(mixed > 0):
                    with pool.Fori(0, nblk) as it:
                        blk = block_of(it, first)
                        u4 = pool.snap((it + nblk * L) * 4)
                        for b in range(2):
                            pool.wait_ge(sm_ready, u4 + (2 * b + 2))
                            nc.gpsimd.tensor_copy(m_ring[:, b, :, :],
                                                  mask_sb[:, :, bass.ds(blk * BLK + b * KT, KT)]) \
                                .then_inc(mask_tile, 1)
                if L < NP:
                    pool.wait_ge(max_split, 5 * (L + 1))
                    for b in range(4):
                        pool.dma_start(m_scr[L, :, :, 32 * b:32 * b + 32].rearrange("j c q -> c j q"),
                                       max_p[32 * b:32 * b + 2 * QT, :, :]).then_inc(max_stored, 16)
                    pool.wait_ge(max_stored, 64 * (L + 1))
                    for h in range(2):
                        r0 = h * HALF + MAX_ROW
                        pool.dma_start(q_st[r0:r0 + PARTS, L, :].rearrange("j (t q) -> j t q", t=QT),
                                       m_scr[L, :, h:2 * QT:2, :]) \
                            .then_inc(max_in, 16)

        @block.scalar
        def _(act):
            for dst, src in ((wk_sb[:, :], wkT), (bk_sb[:, :], bk),
                             (wv_sb[:, :], wvT), (wo_sb[:, :], woT), (wr_sb[:, :], wrT),
                             (bv_sb[:, :], bv.to_broadcast([P, D])), (bo_sb[:, :], bo.to_broadcast([P, D])),
                             (rb_sb[:, :], rb.to_broadcast([P, ER]))):
                act.dma_start(dst, src).then_inc(small_in, 16)
            act.sem_inc(exp_done, 4)
            act.sem_inc(v_evac, 1)
            done = 0

            def step(ins):
                nonlocal done
                done += 1
                ins.then_inc(act_step, 1)

            def std_dev(v_at):
                act.wait_ge(dve_step, v_at)
                step(nc.scalar.activation(st8[:, 3, :], st8[:, 2, :], ACT.Sqrt))

            std_dev(V_XN1 - 2)
            for c in range(QC):
                act.wait_ge(pe_step, c + 1)
                step(nc.scalar.activation(xnT[:, c * 512:(c + 1) * 512], PS[:, c, :], ACT.Copy))
            act.wait_ge(dve_step, V_QPARTS)
            for j in range(PARTS):
                n = PARTS - j
                rows = q_scr[:, K_ROW[j]:K_ROW[j] + HW * n, :].rearrange("h (w i) q -> h w i q", w=HW)
                for i in range(n):
                    act.dma_start(rows[:, :, i, :], q_parts[:, i, :]).then_inc(q_stored, 16)

            act.wait_ge(ctl_ready, 1)
            first = act.value_load(ctl[0:1, 0:1], min_val=0, max_val=NB - 2)
            nblk = act.value_load(ctl[0:1, 2:3], min_val=2, max_val=NB)
            act.wait_ge(consts, N_CONST)
            with act.Fori(0, nblk) as it:
                blk = block_of(it, first)
                act.wait_ge(k_mm, it + 1)
                nc.scalar.activation(k_parts[:, 0, bass.ds(blk * BLK, BLK)], PS[:, 0, 0:BLK], ACT.Identity,
                                     bias=bk_sb[:, :]).then_inc(k_part0, 1)
                act.wait_ge(v_mm, it + 2)
                act.wait_ge(v_stored, it * 16 + 16)
                nc.scalar.activation(v_blk[:, :, :, 0:HW],
                                     PS[:, 1, 0:2 * D].rearrange("p (t h w) -> p t h w", t=2, w=HW),
                                     ACT.Copy).then_inc(v_evac, 1)

            act.wait_ge(q_stored, 16 * 6)
            act.wait_ge(q_zeroed, 2)
            for h in range(2):
                act.dma_start(q_st[h * HALF:h * HALF + MASK_ROW, :, :],
                              q_scr.rearrange("(p h) r q -> h r p q", h=2)[h]).then_inc(q_stacked, 16)

            act.wait_ge(ctx_copied, nblk)
            act.wait_ge(k_mm, nblk)
            nc.scalar.activation(ctx_all[:, :], ctx_all[:, :], ACT.Copy, accum_out=csum[:, :]).then_inc(csum_done, 1)
            act.wait_ge(csum_done, 1)

            for L in range(2, STAGES):
                s = L - 2
                with act.Fori(0, nblk) as it:
                    t2 = act.snap((it + nblk * s) * 2)
                    e8 = act.snap(t2 * 4)
                    for b in range(2):
                        act.wait_ge(tile_done, t2 + (b + 1))
                        for v in range(2 * QC):
                            act.wait_ge(sc_ready, e8 + (4 * b + v + 1))
                            nc.scalar.activation(prob[:, b, v, :], PS[:, v % 2, :],
                                                 ACT.Exp).then_inc(exp_done, 1)
                act.wait_ge(tile_done, nblk * (2 * (s + 1)) + 2)
                nc.scalar.activation(o_sb[:, s, :], PS[:, OB + s % 2, :], ACT.Copy).then_inc(o_evac, 1)

            act.wait_ge(pe_step, 17)
            step(nc.scalar.activation(xnT[:, 0:512], PS[:, 0, :], ACT.Copy))
            std_dev(V_XN2 - 2)
            act.wait_ge(pe_step, 20)
            step(nc.scalar.activation(xnT[:, 0:512], PS[:, 0, :], ACT.Copy))
            act.wait_ge(dve_step, V_GAP)
            step(nc.scalar.activation(rs[:, 3, :], rs[:, 2, :], ACT.Exp))
            assert done == 7, done

            with act.Fori(0, E // 2) as i:
                for b in range(2):
                    for c in range(QC):
                        for ic, (_, n) in enumerate(ICH):
                            k = 6 * b + 3 * c + ic
                            act.wait_ge(gu_ready, i * 12 + (k + 1))
                            nc.scalar.activation(sg[0:n, k % 3, :], PS[0:n, k % 3, :], ACT.Silu) \
                                .then_inc(silu_done, 1)

        @block.tensor
        def _(pe):
            done = 0

            def step(ins):
                nonlocal done
                done += 1
                ins.then_inc(pe_step, 1)

            def transpose_tiles(src, c, bank):
                for j in range(4):
                    last = nc.tensor.transpose(PS[:, bank, j * P:(j + 1) * P], src[:, 4 * c + j, :], ident[:, :])
                step(last)

            pe.sem_inc(y_ready, 2)
            pe.sem_inc(v_mm, 1)
            pe.wait_ge(consts, N_CONST)
            pe.wait_ge(dve_step, V_XN1)
            for c in range(QC):
                transpose_tiles(tmp_b, c, c)
            pe.wait_ge(q_weights, 32)
            for c in range(QC):
                pe.wait_ge(act_step, 2 + c)
                step(nc.tensor.matmul(PS[:, 2 + c, :], wq_sb[:, :], xnT[:, c * 512:(c + 1) * 512],
                                      start=True, stop=True))

            for n, (t0, nt) in enumerate(PIECES):
                pe.wait_ge(mask_in[n], 16)
                for t in range(t0, t0 + nt):
                    for j in range(QT):
                        last = nc.tensor.matmul(PS[:, 4, t:t + 1], mask_f8[:, j, t * KT:(t + 1) * KT],
                                                ones_8[:, :], start=j == 0, stop=j == QT - 1)
            step(last)
            pe.wait_ge(dve_step, V_FLAG)
            step(nc.tensor.transpose(PS[0:NT, 6, 0:P], flag[:, 0, :], ident[:, :]))
            step(nc.tensor.matmul(PS[0:1, 5, 0:2 * NT], ones_f[:, :], flag[:, 1:3, :].rearrange("p a t -> p (a t)"),
                                  start=True, stop=True))

            pe.wait_ge(small_in, 16 * N_SMALL)
            pe.wait_ge(ctl_ready, 1)
            first = pe.value_load(ctl[0:1, 0:1], min_val=0, max_val=NB - 2)
            nblk = pe.value_load(ctl[0:1, 2:3], min_val=2, max_val=NB)
            with pe.Fori(0, nblk) as it:
                blk = block_of(it, first)
                pe.wait_ge(ctx_in, 16)
                pe.wait_ge(k_split, it * 3 + 1)
                nc.tensor.matmul(PS[:, 0, 0:BLK], wk_sb[:, :], ctx_all[:, bass.ds(blk * BLK, BLK)],
                                 start=True, stop=True).then_inc(k_mm, 1)
                pe.wait_ge(ctx_copied, it + 1)
                pe.wait_ge(v_evac, it + 1)
                for t in range(2):
                    last = nc.tensor.matmul(PS[:, 1, t * D:(t + 1) * D], ctx_blk[:, t * KT:(t + 1) * KT],
                                            wv_sb[:, :], start=True, stop=True)
                last.then_inc(v_mm, 1)

            mixed = pe.value_load(ctl[0:1, 1:2], min_val=0, max_val=1)
            pe.wait_ge(k_split, nblk * 3 + 3)
            pe.wait_ge(v_evac, nblk + 1)
            pe.wait_ge(q_stacked, 16 * 2)
            pe.wait_ge(q_rows_in, 32)

            def attention_blocks(L, masked):
                _, exp_at, max_at = pair_slice(L)
                s = L - 2

                def chunk_scores(k_at, e8, b, c):
                    for h in range(2):
                        pe.wait_ge(exp_done, e8 + (4 * b + 2 * c + h + 1 + 2))
                        last = nc.tensor.matmul(PS[:, h, :], k_tile(k_at, b, exp_at)[:, h, :],
                                                q_st[:, s, c * 512:(c + 1) * 512],
                                                start=True, stop=not masked)
                        if masked:
                            for j in range(4):
                                last = nc.tensor.matmul(PS[:, h, j * P:(j + 1) * P],
                                                        m_ring[:, b, 4 * c + j, :], neg_ident[:, :],
                                                        start=False, stop=j == 3)
                        last.then_inc(sc_ready, 1)

                def max_scores(k_at, u4, b, tiles):
                    for t in tiles:
                        u, j = divmod(t, 4)
                        if j == 0:
                            pe.wait_ge(max_done, u4 + (2 * b + u + 1))
                        scores = PS[:, SM + 2 * u + j // 2, j % 2 * BLK:(j % 2 + 1) * BLK]
                        last = nc.tensor.matmul(scores.rearrange("p (h k) -> p h k", h=2),
                                                q_st[:, L, t * P:(t + 1) * P], k_tile(k_at, b, max_at),
                                                start=True, stop=not masked)
                        if masked:
                            for h in range(2):
                                last = nc.tensor.matmul(scores[:, h * KT:(h + 1) * KT],
                                                        neg_ident[:, :], m_ring[:, b, t, :],
                                                        start=False, stop=h == 1)
                        if j == 3:
                            last.then_inc(sm_ready, 1)

                def attention_block(it, first_of_stage):
                    g = pe.snap(it + nblk * L)
                    u4 = pe.snap(g * 4)
                    k_at = pe.snap((g & 1) * 2)
                    e8 = pe.snap((it + nblk * s) * 8) if L >= 2 else None
                    for b in range(2):
                        if b == 0:
                            pe.wait_ge(k_in, g * 32 + 32)
                        if masked:
                            pe.wait_ge(mask_tile, g * 2 + (b + 1))
                        if exp_at is not None:
                            chunk_scores(k_at, e8, b, 0)
                            if b == 1:
                                weighted_values(s, e8 + (4 + 4), e8 * 2 + 16, 0)
                            elif not first_of_stage:
                                weighted_values(s, e8 + 4, e8 * 2, 1)
                            elif s >= 1:
                                weighted_values(s - 1, e8 + 4, e8 * 2, 1)
                        if max_at is not None:
                            max_scores(k_at, u4, b, range(0, 2))
                        elif b == 0:
                            pe.wait_ge(sc_ready, e8 + 2)
                            pe.sem_inc(sm_ready, 1)
                        else:
                            pe.wait_ge(sc_ready, e8 + 4)
                            pe.sem_inc(sm_ready, 1)
                        if exp_at is not None:
                            chunk_scores(k_at, e8, b, 1)
                        if max_at is not None:
                            max_scores(k_at, u4, b, range(2, QT))
                        elif b == 1:
                            pe.wait_ge(sc_ready, e8 + 8)
                            pe.sem_inc(sm_ready, 2)

                attention_block(0, True)
                with pe.Fori(1, nblk) as it:
                    attention_block(it, False)

            def k_tile(k_at, b, use):
                return k_ring[:, :, :, :, b * KT:(b + 1) * KT].rearrange("p a u h k -> p (a u) h k") \
                    [:, bass.ds(k_at + use, 1), :, :].rearrange("p n h k -> p (n h) k")

            def weighted_values(s, exps, loads, b):
                pe.wait_ge(exp_done, exps)
                pe.wait_ge(v_in[b], loads)
                for g in range(4):
                    h, c = divmod(g, 2)
                    last = nc.tensor.matmul(PS[32 * g:32 * g + HW + 1, OB + s % 2, :],
                                            v_ring[:, b, h * (HW + 1):(h + 1) * (HW + 1)],
                                            prob[:, b, 2 * c + h, :],
                                            start=False, stop=True, skip_group_check=True)
                last.then_inc(tile_done, 1)

            def transpose_outputs(s0, n, bank):
                for s in range(s0, s0 + n):
                    transpose_tiles(o_sb[:, s, :].rearrange("p (j q) -> p j q", j=4), 0, bank + s - s0)

            for L in range(STAGES):
                if L == NP:
                    pe.wait_ge(o_evac, 4)
                    pe.wait_ge(max_done, nblk * (4 * NP) + 2)
                    transpose_outputs(0, 4, SM)
                if L == NP + 1:
                    pe.wait_ge(dve_step, V_NORM_A)
                    pe.wait_ge(o_evac, 6)
                    transpose_outputs(4, 2, SM)
                    step(nc.tensor.matmul(PS[:, SM + 2, 0:P], csum_b[:, :], wv_sb[:, :], start=True, stop=True))
                if L >= 2:
                    s = L - 2
                    pe.wait_ge(max_in, 32 * (s + 1))
                    if s >= 2:
                        pe.wait_ge(o_evac, s - 1)
                    nc.tensor.matmul(PS[:, OB + s % 2, :], zeros_b[:, 0:P], zeros_b[:, :], start=True, stop=True,
                                     skip_group_check=True)
                with pe.If(mixed > 0):
                    attention_blocks(L, True)
                with pe.Else():
                    attention_blocks(L, False)
            weighted_values(NP - 1, nblk * (NP * 8) + 4, nblk * (NP * 16), 1)

            pe.wait_ge(o_evac, NP)
            pe.wait_ge(dve_step, V_MEAN)
            transpose_outputs(6, 2, 4)
            pe.wait_ge(dve_step, V_ATT)
            for c in range(QC):
                transpose_tiles(tmp_a, c, c)
            pe.wait_ge(act_step, 4)
            pe.wait_ge(dve_step, V_ATT_T)
            for t in range(QT):
                last = nc.tensor.matmul(PS[:, 2 + t // 4, (t % 4) * P:(t % 4 + 1) * P], xnT[:, t * P:(t + 1) * P],
                                        wo_sb[:, :], start=True, stop=True)
            step(last)
            pe.wait_ge(dve_step, V_XN2)
            for c in range(QC):
                transpose_tiles(tmp_b, c, c)
            pe.wait_ge(act_step, 6)
            pe.wait_ge(dve_step, V_XN2_T)
            for t in range(QT):
                last = nc.tensor.matmul(PS[:, 6, t * ER:(t + 1) * ER], xnT[:, t * P:(t + 1) * P], wr_sb[:, :],
                                        start=True, stop=True)
            step(last)
            assert done == 22, done

            products = ((0, 0), (0, 1), (1, 0))
            pe.wait_ge(dve_step, V_SPLIT)

            def gate_up(i, b, c):
                pe.wait_ge(w_split, i * 6 + (3 * b + 3))
                for ic, (o, n) in enumerate(ICH):
                    k = 6 * b + 3 * c + ic
                    pe.wait_ge(hid_done, i * 12 + (k + 1))
                    for a in range(2):
                        for m, (jw, jx) in enumerate(products):
                            last = nc.tensor.matmul(PS[0:n, 3 * a + k % 3, :],
                                                    w_parts[:, b, jw, a * I + o:a * I + o + n],
                                                    xn_parts[:, jx, c * 512:(c + 1) * 512],
                                                    start=m == 0, stop=m == len(products) - 1)
                    last.then_inc(gu_ready, 1)

            def down(i, b, c):
                pe.wait_ge(hid_done, i * 12 + (6 * b + 3 * c + 3 + 3))
                pe.wait_ge(y_used, i * 4 + (2 * b + c + 1))
                for t in range(4):
                    for ic, (_, n) in enumerate(ICH):
                        last = nc.tensor.matmul(PS[:, 6 + c, t * P:(t + 1) * P],
                                                hid[0:n, c, ic, t * P:(t + 1) * P], w_dn[0:n, b, ic, :],
                                                start=ic == 0, stop=ic == NI - 1)
                last.then_inc(y_ready, 1)

            with pe.Fori(0, E // 2) as i:
                gate_up(i, 0, 0)
                gate_up(i, 0, 1)
                pe.wait_ge(w_in[0], i * 48 + 48)
                down(i, 0, 0)
                gate_up(i, 1, 0)
                pe.wait_ge(w_in[1], i * 48 + 48)
                down(i, 0, 1)
                gate_up(i, 1, 1)
                down(i, 1, 0)
                down(i, 1, 1)

        @block.vector
        def _(dve):
            done = 0

            def step(ins, wait=True):
                nonlocal done
                done += 1
                ins.then_inc(dve_step, 1)
                if wait:
                    dve.wait_ge(dve_step, done)

            def per_tile(v):
                return v.unsqueeze(2).to_broadcast([P, QT, D])

            def mark(value):
                assert done == value, (done, value)

            def layernorm(src, root):
                step(nc.vector.tensor_reduce(st8[:, 0, :], src[:, :, :], AX, ALU.add))
                step(nc.vector.tensor_scalar(st8[:, 1, :], st8[:, 0, :], -1.0 / D, None, ALU.mult))
                step(nc.vector.tensor_tensor(tmp_b[:, :, :], src[:, :, :], per_tile(st8[:, 1, :]), ALU.add))
                step(nc.vector.tensor_tensor(tmp_a[:, :, :], tmp_b[:, :, :], tmp_b[:, :, :], ALU.mult))
                step(nc.vector.tensor_reduce(st8[:, 0, :], tmp_a[:, :, :], AX, ALU.add))
                step(nc.vector.tensor_scalar(st8[:, 2, :], st8[:, 0, :], 1.0 / D, 1e-5, ALU.mult, ALU.add))
                dve.wait_ge(act_step, root)
                step(nc.vector.reciprocal(st8[:, 4, :], st8[:, 3, :]))
                step(nc.vector.tensor_tensor(tmp_b[:, :, :], tmp_b[:, :, :], per_tile(st8[:, 4, :]), ALU.mult))

            dve.sem_inc(k_split, 3)
            dve.wait_ge(x_in, 16)
            layernorm(x_sb, 1)
            mark(V_XN1)

            dve.wait_ge(q_weights, 32)
            dve.wait_ge(pe_step, 4)
            q32 = tmp_b[:, :, :].rearrange("p t d -> p (t d)")
            rest = tmp_a[:, :, :].rearrange("p t d -> p (t d)")
            step(nc.vector.tensor_scalar(q32, PS[:, 2:4, :].rearrange("p c q -> p (c q)"), bq_sb[:, :], None, ALU.add))
            step(nc.vector.tensor_copy(q_parts[:, 0, :], q32))
            step(nc.vector.tensor_tensor(rest, q32, q_parts[:, 0, :], ALU.subtract))
            step(nc.vector.tensor_copy(q_parts[:, 1, :], rest))
            step(nc.vector.tensor_tensor(q_parts[:, 2, :], rest, q_parts[:, 1, :], ALU.subtract))
            mark(V_QPARTS)

            dve.wait_ge(pe_step, 5)
            step(nc.vector.tensor_scalar(flag[:, 0, :], PS[:, 4, 0:NT], (S - 0.5) * BYTE_ONE, None,
                                           ALU.is_ge))
            step(nc.vector.tensor_scalar(flag[:, 1, :], flag[:, 0, :], -1.0, 1.0, ALU.mult, ALU.add))
            step(nc.vector.scalar_tensor_tensor(flag[:, 2, :], PS[:, 4, 0:NT], 0.5 * BYTE_ONE, flag[:, 0, :],
                                                ALU.is_ge, ALU.subtract))
            mark(V_FLAG)
            dve.wait_ge(pe_step, 7)
            step(nc.vector.tensor_scalar(mrow_bf[:, :], PS[0:NT, 6, 0:KT], -BIG, None, ALU.mult))
            mark(V_MROW)
            dve.wait_ge(consts, N_CONST)
            step(nc.vector.tensor_reduce(row[:, 0, :], PS[0:1, 5, 0:2 * NT].rearrange("p (n t) -> p n t", t=2),
                                         AX, ALU.max))
            step(nc.vector.tensor_copy(blk_idx_f[:, :], blk_idx[:, :]))
            step(nc.vector.scalar_tensor_tensor(row[:, 1, 0:NB], row[:, 0, 0:NB], 0.5, blk_idx_f[:, :],
                                                ALU.is_ge, ALU.mult))
            step(nc.vector.tensor_reduce(row[:, 2, 0:1], row[:, 1, 0:NB], AX, ALU.min))
            step(nc.vector.tensor_scalar(ctl[:, 0:1], row[:, 2, 0:1], float(NB - 2), None, ALU.add))
            step(nc.vector.tensor_reduce(row[:, 3, 0:1], row[:, 0, NB:2 * NB], AX, ALU.max))
            step(nc.vector.tensor_scalar(ctl[:, 2:3], row[:, 2, 0:1], -1.0, 2.0, ALU.mult, ALU.add))
            nc.vector.tensor_scalar(ctl[:, 1:2], row[:, 3, 0:1], 0.5, None, ALU.is_ge).then_inc(ctl_ready, 1)

            dve.wait_ge(small_in, 16 * N_SMALL)
            step(nc.vector.tensor_tensor(acc[:, :, :], x_sb[:, :, :],
                                         bo_sb[:, :].unsqueeze(1).to_broadcast([P, QT, D]), ALU.add))
            step(nc.vector.tensor_copy(e_rank_f[:, :], e_rank[:, :]))
            dve.wait_ge(small_in, 16 * N_SMALL)
            dve.wait_ge(ctl_ready, 1)
            first = dve.value_load(ctl[0:1, 0:1], min_val=0, max_val=NB - 2)
            nblk = dve.value_load(ctl[0:1, 2:3], min_val=2, max_val=NB)
            with dve.Fori(0, nblk) as it:
                blk = block_of(it, first)
                it3 = dve.snap(it * 3 + 3)
                cols = bass.ds(blk * BLK, BLK)
                dve.wait_ge(k_part0, it + 1)
                dve.wait_ge(k_split, it3)
                nc.vector.scalar_tensor_tensor(kr1[:, :], PS[:, 0, 0:BLK], bk_sb[:, :], k_parts[:, 0, cols],
                                               ALU.add, ALU.subtract).then_inc(k_split, 1)
                dve.wait_ge(k_split, it3 + 1)
                nc.vector.tensor_copy(k_parts[:, 1, cols], kr1[:, :]).then_inc(k_split, 1)
                dve.wait_ge(k_split, it3 + 2)
                nc.vector.tensor_tensor(k_parts[:, 2, cols], kr1[:, :], k_parts[:, 1, cols], ALU.subtract) \
                    .then_inc(k_split, 1)

            nc.vector.memset(maxT[:, :], 0.0).then_inc(max_init, 1)
            nc.vector.memset(run_max[:, :], FLOOR).then_inc(max_init, 1)
            dve.sem_inc(max_done, 2)
            dve.sem_inc(max_fold, 2)
            for L in range(NP):
                if L:
                    nc.vector.memset(run_max[:, 0:2 * QT], FLOOR).then_inc(max_init, 1)
                dve.wait_ge(max_init, 2 + L)
                with dve.Fori(0, nblk) as it:
                    g = dve.snap(it + nblk * L)
                    u4 = dve.snap(g * 4)
                    dve.wait_ge(max_fold, g * 2 + 2)
                    for b in range(2):
                        for u in range(2):
                            dve.wait_ge(sm_ready, u4 + (2 * b + u + 1 + 4))
                            nc.vector.tensor_reduce(tile_max[:, b, QT * u:QT * (u + 1)],
                                                    PS[:, SM + 2 * u:SM + 2 * u + 2, :]
                                                    .rearrange("p n (m k) -> p (n m) k", k=KT),
                                                    AX, ALU.max).then_inc(max_done, 1)
                    dve.wait_ge(max_done, u4 + 4 + 2)
                    nc.vector.tensor_tensor(tile_max[:, 0, :], tile_max[:, 0, :], tile_max[:, 1, :], ALU.max) \
                        .then_inc(max_fold, 1)
                    dve.wait_ge(max_fold, g * 2 + (1 + 2))
                    nc.vector.tensor_tensor(run_max[:, 0:2 * QT], run_max[:, 0:2 * QT], tile_max[:, 0, :], ALU.max) \
                        .then_inc(max_fold, 1)
                dve.wait_ge(max_fold, nblk * (2 * (L + 1)) + 2)
                nc.vector.transpose(maxT[:, :], run_max[:, :]).then_inc(max_split, 1)
                dve.wait_ge(max_split, 5 * L + 1)
                if L:
                    dve.wait_ge(max_stored, 64 * L)
                nc.vector.tensor_copy(max_p[:, 0, :], maxT[:, :]).then_inc(max_split, 1)
                dve.wait_ge(max_split, 5 * L + 2)
                nc.vector.tensor_tensor(max_r[:, :], maxT[:, :], max_p[:, 0, :], ALU.subtract).then_inc(max_split, 1)
                dve.wait_ge(max_split, 5 * L + 3)
                nc.vector.tensor_copy(max_p[:, 1, :], max_r[:, :]).then_inc(max_split, 1)
                dve.wait_ge(max_split, 5 * L + 4)
                nc.vector.tensor_tensor(max_p[:, 2, :], max_r[:, :], max_p[:, 1, :], ALU.subtract) \
                    .then_inc(max_split, 1)

            dve.wait_ge(csum_done, 1)
            step(nc.vector.tensor_copy(csum_b[:, :], csum[:, :].to_broadcast([P, P])))

            def heads_of(v, h, c, s0, n):
                return v[:, 4 * c:4 * c + 4, 2 * HW * s0:2 * HW * (s0 + n)] \
                    .rearrange("p j (s h w) -> p s j h w", h=2, w=HW)[:, :, :, h, :]

            def of_group(v, h, c, s0, n):
                return v[:, 16 * s0:16 * (s0 + n)].rearrange("p (s j g) -> p s j g", s=n, g=4) \
                    [:, :, :, 2 * h + c].unsqueeze(3).to_broadcast([P, n, 4, HW])

            def normalize(s0, n, bank):
                cols = slice(16 * s0, 16 * (s0 + n))
                o_t = PS[:, bank:bank + n, :].rearrange("p s (m r) -> p (s m) r", r=32)
                step(nc.vector.tensor_scalar(none_l[:, cols], o_t[:, :, HW], 0.0, None, ALU.is_equal))
                step(nc.vector.tensor_tensor(den[:, cols], o_t[:, :, HW], none_l[:, cols], ALU.add))
                step(nc.vector.reciprocal(den[:, cols], den[:, cols]))
                for h in range(2):
                    for c in range(QC):
                        step(nc.vector.tensor_tensor(
                            heads_of(tmp_a, h, c, s0, n),
                            PS[:, bank:bank + n, :].rearrange("p s (j g r) -> p s j g r", j=4, r=32)
                            [:, :, :, 2 * h + c, 0:HW],
                            of_group(den, h, c, s0, n), ALU.mult))

            def add_means(s0, n):
                for h in range(2):
                    for c in range(QC):
                        step(nc.vector.tensor_tensor(
                            heads_of(tmp_b, h, c, s0, n), of_group(none_l, h, c, s0, n),
                            csum_b[:, 2 * HW * s0:2 * HW * (s0 + n)].rearrange("p (s h w) -> p s h w", h=2, w=HW)
                            [:, :, h, :].unsqueeze(2).to_broadcast([P, n, 4, HW]), ALU.mult))
                cols = slice(2 * HW * s0, 2 * HW * (s0 + n))
                step(nc.vector.tensor_tensor(tmp_a[:, :, cols], tmp_a[:, :, cols], tmp_b[:, :, cols], ALU.add))
                step(nc.vector.tensor_tensor(tmp_a[:, :, cols], tmp_a[:, :, cols],
                                             bv_sb[:, cols].unsqueeze(1).to_broadcast([P, QT, 2 * HW * n]), ALU.add))

            dve.wait_ge(pe_step, 11)
            normalize(0, 4, SM)
            mark(V_NORM_A)
            dve.wait_ge(pe_step, 13)
            normalize(4, 2, SM)
            dve.wait_ge(pe_step, 14)
            step(nc.vector.tensor_scalar(csum_b[:, :], PS[:, SM + 2, 0:D], 1.0 / T, None, ALU.mult))
            mark(V_MEAN)
            add_means(0, 6)
            dve.wait_ge(pe_step, 16)
            normalize(6, 2, SM + 2)
            add_means(6, 2)
            mark(V_ATT)
            dve.wait_ge(pe_step, 18)
            step(nc.vector.tensor_copy(xnT[:, 512:1024], PS[:, 1, :]))
            mark(V_ATT_T)
            dve.wait_ge(pe_step, 19)
            flat = acc[:, :, :].rearrange("p t d -> p (t d)")
            step(nc.vector.scalar_tensor_tensor(flat, PS[:, 2:4, :].rearrange("p c q -> p (c q)"),
                                                float(HW) ** -0.5, flat, ALU.mult, ALU.add))
            layernorm(acc, 5)
            mark(V_XN2)
            dve.wait_ge(pe_step, 21)
            step(nc.vector.tensor_copy(xnT[:, 512:1024], PS[:, 1, :]))
            mark(V_XN2_T)
            dve.wait_ge(act_step, 6)
            high = tmp_b[:, :, :].rearrange("p t d -> p (t d)")
            step(nc.vector.tensor_scalar(high.bitcast(I32), xnT[:, :].bitcast(I32), HIGH_BITS, None,
                                         ALU.bitwise_and))
            step(nc.vector.tensor_copy(xn_parts[:, 0, :], high))
            step(nc.vector.tensor_tensor(xn_parts[:, 1, :], xnT[:, :], high, ALU.subtract))
            mark(V_SPLIT)

            def split_weights(b, loads, before):
                dve.wait_ge(w_in[b], loads)
                if before is not None:
                    dve.wait_ge(w_split, before)
                steps = 0 if before is None else before
                nc.vector.tensor_scalar(w_high.bitcast(I32), w_gu[:, b, :].bitcast(I32), HIGH_BITS, None,
                                        ALU.bitwise_and).then_inc(w_split, 1)
                dve.wait_ge(w_split, steps + 1)
                nc.vector.tensor_copy(w_parts[:, b, 0, :], w_high).then_inc(w_split, 1)
                nc.vector.tensor_tensor(w_parts[:, b, 1, :], w_gu[:, b, :], w_high, ALU.subtract) \
                    .then_inc(w_split, 1)

            split_weights(0, 48, None)
            dve.sem_inc(hid_done, 3)
            dve.sem_inc(y_used, 2)

            def per_expert(v):
                return v.unsqueeze(2).to_broadcast([P, QT, ER])

            rank = e_rank_f[:, :].unsqueeze(1).to_broadcast([P, QT, ER])

            def pick(logits, top, hot, tmp):
                step(nc.vector.tensor_reduce(top, logits, AX, ALU.max))
                step(nc.vector.tensor_tensor(hot, logits, per_expert(top), ALU.is_equal))
                step(nc.vector.tensor_tensor(tmp, hot, rank, ALU.mult))
                step(nc.vector.tensor_reduce(rs[:, 1, :], tmp, AX, ALU.max))
                step(nc.vector.tensor_tensor(hot, tmp, per_expert(rs[:, 1, :]), ALU.is_equal))

            dve.wait_ge(pe_step, 22)
            step(nc.vector.tensor_tensor(rt[:, 0, :, :], PS[:, 6, 0:QT * ER].rearrange("p (t e) -> p t e", e=ER),
                                         rb_sb[:, :].unsqueeze(1).to_broadcast([P, QT, ER]), ALU.add))
            pick(rt[:, 0, :, :], rs[:, 0, :], rt[:, 1, :, :], rt[:, 2, :, :])
            step(nc.vector.scalar_tensor_tensor(rt[:, 2, :, :], rt[:, 1, :, :], -BIG, rt[:, 0, :, :],
                                                ALU.mult, ALU.add))
            pick(rt[:, 2, :, :], rs[:, 4, :], rt[:, 3, :, :], rt[:, 4, :, :])
            step(nc.vector.tensor_tensor(rs[:, 2, :], rs[:, 4, :], rs[:, 0, :], ALU.subtract))
            mark(V_GAP)
            dve.wait_ge(act_step, 7)
            step(nc.vector.tensor_scalar(rs[:, 1, :], rs[:, 3, :], 1.0, None, ALU.add))
            step(nc.vector.reciprocal(rs[:, 1, :], rs[:, 1, :]))
            step(nc.vector.tensor_tensor(rs[:, 5, :], rs[:, 3, :], rs[:, 1, :], ALU.mult))
            step(nc.vector.tensor_tensor(rt[:, 1, :, :], rt[:, 1, :, :], per_expert(rs[:, 1, :]), ALU.mult))
            step(nc.vector.tensor_tensor(rt[:, 3, :, :], rt[:, 3, :, :], per_expert(rs[:, 5, :]), ALU.mult))
            step(nc.vector.tensor_tensor(w_all[:, 1:E, :], rt[:, 1, :, :].rearrange("p t e -> p e t"),
                                         rt[:, 3, :, :].rearrange("p t e -> p e t"), ALU.add))
            step(nc.vector.memset(w_all[:, 0, :], 1.0))

            def expert_pair(i, last):
                dve.wait_ge(y_used, i * 4 + 2)
                nc.vector.tensor_copy(w_cur[:, :, :], w_all[:, bass.ds(i * 2, 2), :]).then_inc(w_copied, 1)

                def hidden(b, c):
                    dve.wait_ge(y_ready, i * 4 + (2 * b + c + 1))
                    for ic, (_, n) in enumerate(ICH):
                        k = 6 * b + 3 * c + ic
                        dve.wait_ge(silu_done, i * 12 + (k + 1))
                        nc.vector.tensor_tensor(hid[0:n, c, ic, :], sg[0:n, k % 3, :], PS[0:n, 3 + k % 3, :],
                                                ALU.mult).then_inc(hid_done, 1)

                def add_output(b, c):
                    dve.wait_ge(y_ready, i * 4 + (2 * b + c + 1 + 2))
                    dve.wait_ge(y_used, i * 4 + (2 * b + c + 1))
                    for t in range(4):
                        tile = acc[:, 4 * c + t, :]
                        ins = nc.vector.scalar_tensor_tensor(tile, PS[:, 6 + c, t * P:(t + 1) * P],
                                                             w_cur[:, b, 4 * c + t:4 * c + t + 1], tile,
                                                             ALU.mult, ALU.add)
                    ins.then_inc(y_used, 1)

                hidden(0, 0)
                split_weights(1, i * 48 + 48, i * 6 + 3)
                hidden(0, 1)
                dve.wait_ge(w_copied, i + 1)
                add_output(0, 0)
                hidden(1, 0)
                add_output(0, 1)
                hidden(1, 1)
                if not last:
                    split_weights(0, i * 48 + 96, i * 6 + 6)
                add_output(1, 0)
                add_output(1, 1)

            with dve.Fori(0, E // 2 - 1) as i:
                expert_pair(i, False)
            expert_pair(E // 2 - 1, True)


def kernel(**inputs):
    import numpy as np
    import concourse.bacc as bacc
    from concourse.bass_utils import run_bass_kernel_spmd as run

    a = {n: np.asarray(v) for n, v in inputs.items()}
    at, ff = "L0_xattn_", "L0_ffn_"
    x = a["x"][0]
    S, D = x.shape
    T = a["ctx_1024"].shape[1]
    front = padded_keys(T) - T
    I = a[ff + "sg"].shape[0]
    g = np.concatenate([a[ff + "sg"][None], a[ff + "rg"]]).transpose(0, 2, 1)
    u = np.concatenate([a[ff + "su"][None], a[ff + "ru"]]).transpose(0, 2, 1)
    arrays = {
        "x": x,
        "ctxT": np.pad(a["ctx_1024"][0].T, ((0, 0), (front, 0))),
        "mask": np.pad(a["mask_SxS2_bk1"], ((0, 0), (front, 0)), constant_values=True),
        "wqT": a[at + "Wq"].reshape(D, D).T, "bq": a[at + "bq"].reshape(D, 1),
        "wkT": a[at + "Wk"].reshape(D, D).T, "bk": a[at + "bk"].reshape(D, 1),
        "wvT": a[at + "Wv"].reshape(D, D).T, "bv": a[at + "bv"].reshape(1, D),
        "woT": a[at + "Wo"].reshape(D, D).T, "bo": a[at + "bo"].reshape(1, D),
        "gu": np.concatenate([g, u], axis=2),
        "dn": np.concatenate([a[ff + "sd"][None], a[ff + "rd"]]).transpose(0, 2, 1),
        "wrT": a[ff + "wr"].T, "rb": a[ff + "rb"].reshape(1, -1),
    }
    arrays = {n: np.ascontiguousarray(v) for n, v in arrays.items()}
    nc = bacc.Bacc("TRN2", target_bir_lowering=False, num_devices=1)
    args = {n: nc.dram_tensor(f"in_{n}", v.shape, mybir.dt.from_np(v.dtype), kind="ExternalInput").ap()
            for n, v in arrays.items()}
    out = nc.dram_tensor("out", (1, S, D), F32, kind="ExternalOutput").ap()
    xattn_moe(nc, *args.values(), out, T)
    r = run(nc, [{f"in_{n}": v for n, v in arrays.items()}], core_ids=[0])
    return r.results[0]["out"]
```
